# Optimizing a Trainium2 kernel written in Bass

```python
import numpy as np
import jax
import jax.numpy as jnp

def _softmax(x, axis=-1):
    return jax.nn.softmax(x, axis=axis)

def _gelu(x):
    return jax.nn.gelu(x, approximate=True)

def _silu(x):
    return jax.nn.silu(x)

def _sigmoid(x):
    return jax.nn.sigmoid(x)

def _layernorm(x, axis=-1, eps=1e-05):
    m = jnp.mean(x, axis=axis, keepdims=True)
    v = jnp.var(x, axis=axis, keepdims=True)
    return (x - m) / jnp.sqrt(v + eps)

def _scatter_add(tgt, idx, src, axis=0):
    return tgt.at[idx].add(src)

def _segment_sum(src, seg, n):
    return jax.ops.segment_sum(src, seg, n)
kernel_name = 'mk_adj_preln_d2_adj_r2_d3e357'

def setup_inputs(seed: int=0):
    np.random.seed(seed)
    _w = jnp.asarray

    def _rec_inputs():
        import jax
        import jax.numpy as jnp
        _gk = jax.random.key(seed)
        x = -0.0002928 + 1 * jax.random.normal(jax.random.fold_in(_gk, 1), (128, 64, 256), jnp.float32)
        _w = (1.0 + jnp.arange(64, dtype=jnp.float32)) ** (-0.5)
        _w = _w / _w.mean()
        _pij = jnp.clip(0.0625 * _w[:, None] * _w[None, :], 0.0, 1.0)
        _a = jax.random.uniform(jax.random.fold_in(_gk, 2), (128, 64, 64)) < _pij
        adj = _a.astype(jnp.int32)
        return (x, adj)
    x, adj = _rec_inputs()

    def _L0_gnn_setup():
        import jax, jax.numpy as jnp
        import numpy as np
        L = 3
        D = 256
        B, N = (8, 512)
        EPS = 1e-05

        def layernorm(x, gamma, beta):
            mu = jnp.mean(x, axis=-1, keepdims=True)
            var = jnp.var(x, axis=-1, keepdims=True)
            return (x - mu) * jax.lax.rsqrt(var + EPS) * gamma + beta
        key = jax.random.key(seed)
        ks = jax.random.split(key, 12)
        s = 1.0 / np.sqrt(D)
        node_features = jax.random.normal(ks[0], (B, N, D), dtype=jnp.float32)
        adjacency_matrix = jax.random.randint(ks[1], (B, N, N), 0, 2, dtype=jnp.int32)
        return {'node_features': node_features, 'adjacency_matrix': adjacency_matrix, 'attn_w': jax.random.normal(ks[2], (L, 2 * D), dtype=jnp.float32) * (1.0 / np.sqrt(2 * D)), 'attn_b': jax.random.normal(ks[3], (L,), dtype=jnp.float32) * 0.01, 'W1': jax.random.normal(ks[4], (L, D, 4 * D), dtype=jnp.float32) * s, 'b1': jnp.zeros((L, 4 * D), dtype=jnp.float32), 'W2': jax.random.normal(ks[5], (L, 4 * D, D), dtype=jnp.float32) * (1.0 / np.sqrt(4 * D)), 'b2': jnp.zeros((L, D), dtype=jnp.float32), 'g1': jnp.ones((L, D), dtype=jnp.float32), 'beta1': jnp.zeros((L, D), dtype=jnp.float32), 'g2': jnp.ones((L, D), dtype=jnp.float32), 'beta2': jnp.zeros((L, D), dtype=jnp.float32)}
    _L0_gnn_all = _L0_gnn_setup()
    _L0_gnn_in = {k: v for k, v in _L0_gnn_all.items() if k in ('attn_w', 'attn_b', 'W1', 'b1', 'W2', 'b2', 'g1', 'beta1', 'g2', 'beta2')}
    del _L0_gnn_all

    def _L1_gnn_setup():
        import jax, jax.numpy as jnp
        import numpy as np
        B, N, D = (32, 128, 256)
        DIR = 2
        NUM_LABELS = 16
        key = jax.random.key(seed)
        k1, k2, k3, k4 = jax.random.split(key, 4)
        feature = jax.random.normal(k1, (B, N, D), dtype=jnp.float32)
        graph = jax.random.randint(k2, (B, N, N), 0, NUM_LABELS, dtype=jnp.int64)
        weights = jax.random.normal(k3, (DIR, D, D), dtype=jnp.float32) * (1.0 / np.sqrt(D))
        stdv = 1.0 / np.sqrt(D)
        bias = jax.random.uniform(k4, (NUM_LABELS, D), dtype=jnp.float32, minval=-stdv, maxval=stdv)
        return {'feature': feature, 'graph': graph, 'weights': weights, 'bias': bias}
    _L1_gnn_all = _L1_gnn_setup()
    _L1_gnn_in = {k: v for k, v in _L1_gnn_all.items() if k in ('weights', 'bias')}
    del _L1_gnn_all
    return {'x': x, 'adj': adj, 'L0_gnn_attn_w': _L0_gnn_in['attn_w'], 'L0_gnn_attn_b': _L0_gnn_in['attn_b'], 'L0_gnn_W1': _L0_gnn_in['W1'], 'L0_gnn_b1': _L0_gnn_in['b1'], 'L0_gnn_W2': _L0_gnn_in['W2'], 'L0_gnn_b2': _L0_gnn_in['b2'], 'L0_gnn_g1': _L0_gnn_in['g1'], 'L0_gnn_beta1': _L0_gnn_in['beta1'], 'L0_gnn_g2': _L0_gnn_in['g2'], 'L0_gnn_beta2': _L0_gnn_in['beta2'], 'L1_gnn_weights': _L1_gnn_in['weights'], 'L1_gnn_bias': _L1_gnn_in['bias']}

def reference(x, adj, L0_gnn_attn_w, L0_gnn_attn_b, L0_gnn_W1, L0_gnn_b1, L0_gnn_W2, L0_gnn_b2, L0_gnn_g1, L0_gnn_beta1, L0_gnn_g2, L0_gnn_beta2, L1_gnn_weights, L1_gnn_bias):
    import jax
    import jax.numpy as jnp

    def _L0_gnn_ref(node_features, adjacency_matrix, attn_w, attn_b, W1, b1, W2, b2, g1, beta1, g2, beta2):
        import jax, jax.numpy as jnp
        import numpy as np
        L = 3
        D = 256
        B, N = (8, 512)
        EPS = 1e-05

        def layernorm(x, gamma, beta):
            mu = jnp.mean(x, axis=-1, keepdims=True)
            var = jnp.var(x, axis=-1, keepdims=True)
            return (x - mu) * jax.lax.rsqrt(var + EPS) * gamma + beta
        n = adjacency_matrix.shape[-1]
        mask = adjacency_matrix.astype(jnp.float32) + jnp.eye(n, dtype=jnp.float32) > 0
        x = node_features
        d = x.shape[-1]
        for l in range(attn_w.shape[0]):
            si = x @ attn_w[l, :d]
            sj = x @ attn_w[l, d:]
            scores = si[:, :, None] + sj[:, None, :] + attn_b[l]
            scores = jnp.where(scores >= 0, scores, 0.2 * scores)
            scores = jnp.where(mask, scores, -jnp.inf)
            attn = jax.nn.softmax(scores, axis=-1)
            agg = jnp.einsum('bij,bjd->bid', attn, x)
            h = layernorm(x + agg, g1[l], beta1[l])
            ff = jax.nn.gelu(h @ W1[l] + b1[l], approximate=False) @ W2[l] + b2[l]
            x = layernorm(h + ff, g2[l], beta2[l])
        return x

    def _L1_gnn_ref(feature, graph, weights, bias):
        import jax, jax.numpy as jnp
        import numpy as np
        B, N, D = (32, 128, 256)
        DIR = 2
        NUM_LABELS = 16
        out = feature + jnp.einsum('bni,doi->bno', feature, weights)
        out = out + jnp.take(bias, graph, axis=0).sum(axis=2)
        return out
    h = jnp.maximum(_layernorm(x, axis=-1), 0.0)
    x = x + _L0_gnn_ref(h, adj, L0_gnn_attn_w, L0_gnn_attn_b, L0_gnn_W1, L0_gnn_b1, L0_gnn_W2, L0_gnn_b2, L0_gnn_g1, L0_gnn_beta1, L0_gnn_g2, L0_gnn_beta2)
    h = jnp.maximum(_layernorm(x, axis=-1), 0.0)
    x = x + _L1_gnn_ref(h, adj, L1_gnn_weights, L1_gnn_bias)
    return x

_drawn_inputs = setup_inputs


def setup_inputs(seed=0):
    import zlib

    import numpy as np

    out = dict(_drawn_inputs(seed))
    spreads = {'L0_gnn_b1': (0.0, 0.1),
     'L0_gnn_b2': (0.0, 0.1),
     'L0_gnn_g1': (1.0, 0.2),
     'L0_gnn_beta1': (0.0, 0.1),
     'L0_gnn_g2': (1.0, 0.2),
     'L0_gnn_beta2': (0.0, 0.1)}
    factors = {'L0_gnn_attn_b': 64.0}
    for name, (base, spread) in spreads.items():
        noise = np.random.default_rng([zlib.crc32(name.encode()), seed]).standard_normal(out[name].shape)
        drawn = base * np.exp(spread * noise) if base else spread * noise
        out[name] = jnp.asarray(drawn.astype(out[name].dtype))
    for name, factor in factors.items():
        out[name] = (out[name] * factor).astype(out[name].dtype)
    return out
```

```python
from contextlib import ExitStack

import concourse.bass as bass
from concourse import mybir

F32 = mybir.dt.float32
F16 = mybir.dt.float16
I32 = mybir.dt.int32
ALU = mybir.AluOpType
ACT = mybir.ActivationFunctionType
AX_X = mybir.AxisListType.X

P = 128
N = 64
D = 256
K = D // P
F = 4 * D
C = F // P
L = 3
LABELS = 16
R = 4
ROWS = R * P
EPS = 1e-5
SLOPE = 0.2
MASKED = -1e30
SA = 16.0
SP = 256.0
SW = 64.0
SL = 16.0
FFN_LAG = 2


class Unit:

    def __init__(self, T, k, groups):
        self.dt, self.p = k // L, k % L
        self.T, self.groups = T, groups
        self.fixed = isinstance(T, int)

    def there(self, before=0):
        return not self.fixed or 0 <= self.T + self.dt - before - self.p < self.groups

    def group(self):
        return self.T + (self.dt - self.p)

    def done(self, each, n=0, before=0):
        dt = self.dt - before
        if not self.fixed:
            return self.T * (L * each) + ((L * dt + self.p - L) * each + n)
        t = self.T + dt
        units = sum(0 <= s // L - s % L < self.groups for s in range(L * t + self.p))
        return units * each + (n if self.there(before) else 0)


def gnn_block(nc, x, adj, adjt_g, attn_w, attn_b, w1, b1, w2, b2, g1, g1_row, beta1, beta1_row, g2, beta2, wl, lab, out):
    G = x.shape[0] // ROWS

    x_g = x.rearrange("(g r p) d -> g p r d", r=R, p=P)
    adj_g = adj.rearrange("(g r p) n -> g p r n", r=R, p=P)
    out_g = out.rearrange("(g r p) d -> g p r d", r=R, p=P)

    ctx = ExitStack()
    with ctx:
        def sb(name, shape, dt=F32):
            return ctx.enter_context(nc.sbuf_tensor(name, shape, dt))

        def psum(name, shape, dt=F32):
            return ctx.enter_context(nc.psum_tensor(name, shape, dt))

        def sem(name):
            return ctx.enter_context(nc.semaphore(name))

        w1_hi = sb("w1_hi", [P, L, K, F], F16)
        w1_lo = sb("w1_lo", [P, L, K, F], F16)
        w2_hi = sb("w2_hi", [P, L, C, D], F16)
        w2_lo = sb("w2_lo", [P, L, C, D], F16)
        wl_hi = sb("wl_hi", [P, K, D], F16)
        wl_lo = sb("wl_lo", [P, K, D], F16)
        lab_hi = sb("lab_hi", [LABELS, D], F16)
        lab_lo = sb("lab_lo", [LABELS, D], F16)
        stage1 = sb("stage1", [P, K, F])
        stage2 = sb("stage2", [P, C, D])
        lab_f = sb("lab_f", [LABELS, D])
        g1_r = sb("g1_r", [P, L, D])
        c1_r = sb("c1_r", [P, L, D])
        b2_r = sb("b2_r", [P, L, D])
        g2_r = sb("g2_r", [P, L, D])
        beta2_r = sb("beta2_r", [P, L, D])
        attn_r = sb("attn_r", [P, L, 2, D])
        attn_b_r = sb("attn_b_r", [P, L])
        g1_c = sb("g1_c", [P, L, K])
        g1_s = sb("g1_s", [P, L, K])
        beta1_c = sb("beta1_c", [P, L, K])
        b1_c = sb("b1_c", [P, L, C])
        b1_f = sb("b1_f", [P, L, C])
        ident = sb("ident", [P, P], F16)
        blocks = sb("blocks", [P, P])
        delta = sb("delta", [P, N])
        wl_eye = sb("wl_eye", [P, K, D])
        labels = sb("labels", [P, LABELS // 2])
        pick = sb("pick", [P, LABELS // 2, LABELS], F16)
        half = sb("half", [P, R])
        x_in = sb("x_in", [P, R, D])
        x_again = sb("x_again", [P, R, D])
        adj_in = sb("adj_in", [P, R, N], I32)
        adjt_in = sb("adjt_in", [P, ROWS], I32)
        adj_f = sb("adj_f", [P, R, N])
        off = [sb(f"off{i}", [P, R, N]) for i in range(L + 1)]
        OFF_OF = (0, 1, 3)
        xs = [sb(f"xs{p}", [P, R, D]) for p in range(L)]
        x_hi = sb("x_hi", [P, R, D], F16)
        x_lo = sb("x_lo", [P, R, D], F16)
        s_ij = sb("s_ij", [P, L, 2, R])
        dots_junk = sb("dots_junk", [P, 2, D])
        diag = sb("diag", [P, R, N])
        score = sb("score", [P, R, N])
        leaky = sb("leaky", [P, R, N])
        row_max = sb("row_max", [P, R])
        shifted = sb("shifted", [P, R, N])
        expd = sb("expd", [P, R, N])
        row_sum = sb("row_sum", [P, R])
        row_sum_s = sb("row_sum_s", [P, R])
        inv_sum = sb("inv_sum", [P, L, R])
        p_hi = sb("p_hi", [P, R, P], F16)
        p_lo = sb("p_lo", [P, R, P], F16)
        pt = sb("pt", [P, 2, R, P], F16)
        u = sb("u", [P, R, D])
        h = sb("h", [P, R, D])
        h_hi = sb("h_hi", [P, R, D], F16)
        h_lo = sb("h_lo", [P, R, D], F16)
        ht = [sb(f"ht{p}", [P, 2, K, ROWS], F16) for p in range(L)]
        hb = [sb(f"hb{p}", [P, R, D]) for p in range(L)]
        act32 = sb("act32", [P, 2, ROWS])
        act_hi = sb("act_hi", [P, 4, ROWS], F16)
        act_lo = sb("act_lo", [P, 4, ROWS], F16)
        y = sb("y", [P, R, D])
        xn = sb("xn", [P, R, D])
        LN_Y, LN_U, LN_IN, LN_LAST = range(4)
        stats = sb("stats", [P, 4, R, 6])
        mv = sb("mv", [P, 4, R, 2])
        var = sb("var", [P, 4, R])
        rstd = sb("rstd", [P, 4, R])
        x2 = sb("x2", [P, R, D])
        r_hi = sb("r_hi", [P, R, D], F16)
        r_lo = sb("r_lo", [P, R, D], F16)
        rt = sb("rt", [P, 2, K, ROWS], F16)
        adjt_h = sb("adjt_h", [P, ROWS], F16)
        onehot = stage2[:, :, :].bitcast(F16).rearrange("p l (s d) -> p (l s d)", s=2).rearrange("p (l r) -> p l r", r=ROWS)
        counts = sb("counts", [LABELS, ROWS], F16)
        last_n = stage1[:, 0, :].rearrange("p (r d) -> p r d", r=R)
        result = stage1[:, 1, :].rearrange("p (r d) -> p r d", r=R)

        ps_h = [psum(f"ps_h{i}", [P, ROWS]) for i in range(2)]
        ps_f = [psum(f"ps_f{i}", [P, 2, D]) for i in range(2)]
        ps_a = [psum(f"ps_a{i}", [P, 2, D]) for i in range(2)]
        ps_s = psum("ps_s", [P, K, ROWS], F16)
        ps_t = psum("ps_t", [P, 2 * ROWS], F16)
        ps_s32 = ps_s[:, :, :].rearrange("p k r -> p (k r)").bitcast(F32)

        consts_in = sem("consts_in")
        stage1_in = sem("stage1_in")
        stage2_in = sem("stage2_in")
        lab_in = sem("lab_in")
        x_loaded = sem("x_loaded")
        adj_loaded = sem("adj_loaded")
        x_again_loaded = sem("x_again_loaded")
        adjt_loaded = sem("adjt_loaded")
        stored = sem("stored")
        masks = sem("masks")
        halves_set = sem("halves_set")
        c1_ready = sem("c1_ready")
        g1s_ready = sem("g1s_ready")
        w1_hi_ready = sem("w1_hi_ready")
        w1_lo_ready = sem("w1_lo_ready")
        w2_hi_ready = sem("w2_hi_ready")
        w2_lo_ready = sem("w2_lo_ready")
        b1_summed = sem("b1_summed")
        b1_ready = sem("b1_ready")
        wl_steps = sem("wl_steps")
        wl_hi_ready = sem("wl_hi_ready")
        wl_ready = sem("wl_ready")
        in_stats = sem("in_stats")
        in_mv = sem("in_mv")
        in_var = sem("in_var")
        in_rstd = sem("in_rstd")
        in_norm = sem("in_norm")
        in_ready = sem("in_ready")
        adj_f_ready = sem("adj_f_ready")
        off_ready = [sem(f"off_ready{i}") for i in range(L + 1)]
        dots_ready = sem("dots_ready")
        diag_ready = sem("diag_ready")
        spread = sem("spread")
        scored = sem("scored")
        leaked = sem("leaked")
        max_ready = sem("max_ready")
        shift_ready = sem("shift_ready")
        exp_ready = sem("exp_ready")
        sum_ready = sem("sum_ready")
        sum_scaled = sem("sum_scaled")
        inv_ready = sem("inv_ready")
        p_hi_ready = sem("p_hi_ready")
        p_lo_ready = sem("p_lo_ready")
        p_turned = sem("p_turned")
        pt_ready = sem("pt_ready")
        x_hi_ready = sem("x_hi_ready")
        x_lo_ready = sem("x_lo_ready")
        mixed = sem("mixed")
        u_ready = sem("u_ready")
        u_stats = sem("u_stats")
        u_mv = sem("u_mv")
        u_var = sem("u_var")
        u_rstd = sem("u_rstd")
        h_ready = sem("h_ready")
        h_hi_ready = sem("h_hi_ready")
        h_lo_ready = sem("h_lo_ready")
        h_turned = sem("h_turned")
        ht_ready = sem("ht_ready")
        hg_ready = sem("hg_ready")
        hb_ready = sem("hb_ready")
        hidden = sem("hidden")
        act_ready = sem("act_ready")
        act_hi_ready = sem("act_hi_ready")
        act_lo_ready = sem("act_lo_ready")
        second = sem("second")
        y_ready = sem("y_ready")
        y_stats = sem("y_stats")
        y_mv = sem("y_mv")
        y_var = sem("y_var")
        y_rstd = sem("y_rstd")
        xn_ready = sem("xn_ready")
        xg_ready = sem("xg_ready")
        x_ready = sem("x_ready")
        x2_ready = sem("x2_ready")
        last_stats = sem("last_stats")
        last_mv = sem("last_mv")
        last_var = sem("last_var")
        last_rstd = sem("last_rstd")
        last_norm = sem("last_norm")
        r_hi_ready = sem("r_hi_ready")
        r_lo_ready = sem("r_lo_ready")
        r_turned = sem("r_turned")
        rt_ready = sem("rt_ready")
        adjt_h_ready = sem("adjt_h_ready")
        onehot_ready = sem("onehot_ready")
        counted = sem("counted")
        counts_ready = sem("counts_ready")
        mapped = sem("mapped")
        result_ready = sem("result_ready")

        MASK_STEPS = 6
        CONSTS = 10
        FIRST_T, LAST_PREP_T = -1, 0

        def program(eng, body):
            for T in range(FIRST_T, L):
                body(T)
            with eng.Fori(L, G - 1) as T:
                body(T)
            for T in range(G - 1, G + L):
                body(T)

        def entry(T):
            return T + 1 if not isinstance(T, int) or 0 <= T + 1 < G else None

        def last(T):
            return T - L if not isinstance(T, int) or 0 <= T - L < G else None

        def more(T, n):
            return not isinstance(T, int) or 0 <= n < G

        def groups_before(n):
            return min(max(n, 0), G) if isinstance(n, int) else n

        def upto(v, each):
            return v.done(each, each)

        block = ctx.enter_context(nc.Block())

        def wait(eng, semaphore, value):
            if not isinstance(value, int) or value > 0:
                eng.wait_ge(semaphore, value)

        @block.sync
        def _(sp):
            def load_constants():
                for tile, row in ((g1_c, g1), (beta1_c, beta1), (b1_c, b1)):
                    sp.dma_start(tile[:, :, :], row).then_inc(consts_in, 16)
                sp.dma_start(attn_r[:, :, :, :].rearrange("p l s d -> p (l s d)"), attn_w.to_broadcast([P, L * 2 * D])).then_inc(consts_in, 16)
                sp.dma_start(attn_b_r[:, :], attn_b.to_broadcast([P, L])).then_inc(consts_in, 16)
                for tile, row in ((g1_r, g1_row), (c1_r, beta1_row), (b2_r, b2), (g2_r, g2), (beta2_r, beta2)):
                    sp.dma_start(tile[:, :, :].rearrange("p l d -> p (l d)"), row.to_broadcast([P, L * D])).then_inc(consts_in, 16)
                for l in range(L):
                    wait(sp, w1_lo_ready, K * l)
                    wait(sp, b1_summed, l)
                    sp.dma_start(stage1[:, :, :], w1[l].rearrange("(k p) f -> p k f", p=P)).then_inc(stage1_in, 16)
                    wait(sp, w2_lo_ready, l)
                    sp.dma_start(stage2[:, :, :], w2[l].rearrange("(c p) d -> p c d", p=P)).then_inc(stage2_in, 16)
                sp.wait_ge(w2_lo_ready, L)
                sp.dma_start(stage2[:, 0:2 * K, :], wl).then_inc(stage2_in, 16)
                sp.dma_start(lab_f[:, :], lab).then_inc(lab_in, 16)

            def body(T):
                e, g = entry(T), last(T)
                if e is not None:
                    wait(sp, in_ready, e)
                    sp.dma_start(x_in[:, :, :], x_g[e]).then_inc(x_loaded, 16)
                    wait(sp, adj_f_ready, e)
                    sp.dma_start(adj_in[:, :, :], adj_g[e]).then_inc(adj_loaded, 16)
                if isinstance(T, int) and T == FIRST_T:
                    load_constants()
                n = T - L + 1
                if more(T, n):
                    wait(sp, x2_ready, n)
                    sp.dma_start(x_again[:, :, :], x_g[n]).then_inc(x_again_loaded, 16)
                    wait(sp, adjt_h_ready, n)
                    for s in range(2):
                        sp.dma_start(adjt_in[s * N:(s + 1) * N, :], adjt_g[n]).then_inc(adjt_loaded, 16)
                if g is not None:
                    sp.wait_ge(result_ready, g * 2 + 2)
                    sp.dma_start(out_g[g], result[:, :, :]).then_inc(stored, 16)

            program(sp, body)
            sp.wait_ge(stored, 16 * G)

        @block.gpsimd
        def _(pool):
            def mark(view, pattern, base):
                return nc.gpsimd.affine_select(out=view, in_=view, compare_op=ALU.not_equal, fill=1.0, base=base,
                                               pattern=pattern, channel_multiplier=1)

            nc.gpsimd.memset(half[:, :], -0.5)
            nc.gpsimd.memset(delta[:, :], 0.0)
            nc.gpsimd.memset(ident[:, :], 0.0)
            nc.gpsimd.memset(wl_eye[:, :, :], 0.0)
            nc.gpsimd.memset(blocks[:, :], 0.0)
            nc.gpsimd.memset(pick[:, :, :], 0.0)
            nc.gpsimd.memset(p_hi[:, :, :], 0.0)
            nc.gpsimd.memset(p_lo[:, :, :], 0.0).then_inc(masks, 1)
            pool.wait_ge(masks, 1)
            mark(delta[:, :], [[-1, N]], 0).then_inc(masks, 1)
            pool.wait_ge(masks, 2)
            mark(delta[:, :], [[-1, N]], -N).then_inc(masks, 1)
            mark(ident[:, :], [[-1, P]], 0).then_inc(masks, 1)
            mark(wl_eye[:, 0, :], [[-1, D]], 0).then_inc(masks, 1)
            mark(wl_eye[:, 1, :], [[-1, D]], P).then_inc(masks, 1)
            pool.wait_ge(consts_in, 16 * CONSTS)
            nc.gpsimd.tensor_tensor(c1_r[:, :, :], c1_r[:, :, :], b2_r[:, :, :], ALU.add).then_inc(c1_ready, 1)
            pool.wait_ge(c1_ready, 1)
            pool.wait_ge(masks, MASK_STEPS)

            def rows_of(tile, l):
                return tile[:, l, :].unsqueeze(1).to_broadcast([P, R, D])

            def inverse_root(ln):
                return nc.gpsimd.tensor_tensor(rstd[:, ln, :], var[:, ln, :], half[:, :], ALU.pow)

            def body(T):
                e, g = entry(T), last(T)
                for j in range(L):
                    v, w = Unit(T, j - 1, G), Unit(T, j + 1, G)
                    if v.there():
                        pool.wait_ge(y_var, v.done(1, 1))
                        inverse_root(LN_Y).then_inc(y_rstd, 1)
                    if j == 1 and g is not None:
                        pool.wait_ge(last_var, g + 1)
                        inverse_root(LN_LAST).then_inc(last_rstd, 1)
                    if w.there():
                        pool.wait_ge(u_var, w.done(1, 1))
                        inverse_root(LN_U).then_inc(u_rstd, 1)
                    if j == 0 and e is not None:
                        pool.wait_ge(in_var, e + 1)
                        inverse_root(LN_IN).then_inc(in_rstd, 1)
                    if v.there():
                        pool.wait_ge(xn_ready, v.done(R, R))
                        if v.p < L - 1:
                            to = xs[v.p + 1]
                            wait(pool, u_ready, Unit(T, j + 3, G).done(R, R, before=1))
                        else:
                            to = x2
                            wait(pool, result_ready, g * 2)
                        nc.gpsimd.tensor_tensor(to[:, :, :], xn[:, :, :], rows_of(g2_r, v.p), ALU.mult).then_inc(xg_ready, 1)
                        pool.wait_ge(xg_ready, v.done(1, 1))
                        nc.gpsimd.tensor_tensor(to[:, :, :], to[:, :, :], rows_of(beta2_r, v.p), ALU.add).then_inc(x_ready, 1)
                    if v.there() and v.p == L - 1:
                        pool.wait_ge(x_ready, v.done(1, 1))
                        pool.wait_ge(x_again_loaded, g * 16 + 16)
                        nc.gpsimd.tensor_tensor(x2[:, :, :], x2[:, :, :], x_again[:, :, :], ALU.add).then_inc(x2_ready, 1)
                    if w.there():
                        pool.wait_ge(h_ready, w.done(R, R))
                        wait(pool, y_ready, w.done(2, 2, before=1))
                        nc.gpsimd.tensor_tensor(hb[w.p][:, :, :], h[:, :, :], rows_of(g1_r, w.p), ALU.mult).then_inc(hg_ready, 1)
                        pool.wait_ge(hg_ready, w.done(1, 1))
                        nc.gpsimd.tensor_tensor(hb[w.p][:, :, :], hb[w.p][:, :, :], rows_of(c1_r, w.p), ALU.add).then_inc(hb_ready, 1)

            program(pool, body)

        @block.scalar
        def _(act):
            def prepare(l):
                act.wait_ge(g1s_ready, 1)
                act.wait_ge(stage1_in, 16 * (l + 1))
                for k in range(K):
                    nc.scalar.activation(w1_hi[:, l, k, :], stage1[:, k, :], ACT.Copy,
                                         scale=g1_s[:, l, k:k + 1]).then_inc(w1_hi_ready, 1)
                act.wait_ge(stage2_in, 16 * (l + 1))
                nc.scalar.activation(w2_hi[:, l, :, :], stage2[:, :, :], ACT.Copy, scale=SW).then_inc(w2_hi_ready, 1)

            def prepare_last():
                act.wait_ge(wl_steps, 2)
                nc.scalar.activation(wl_hi[:, :, :], wl_eye[:, :, :], ACT.Copy, scale=SL).then_inc(wl_hi_ready, 1)
                act.wait_ge(lab_in, 16)
                nc.scalar.activation(lab_hi[:, :], lab_f[:, :], ACT.Copy, scale=SL).then_inc(wl_hi_ready, 1)

            def body(T):
                e, g = entry(T), last(T)
                for j in range(L):
                    now, w, s = Unit(T, j, G), Unit(T, j + 1, G), Unit(T, j + 2, G)
                    if isinstance(T, int) and T == FIRST_T:
                        prepare(j)
                    if isinstance(T, int) and T == LAST_PREP_T and j == L - 1:
                        prepare_last()
                    for c in range(C):
                        if now.there():
                            if now.fixed and c == 0:
                                act.wait_ge(b1_ready, now.p + 1)
                            act.wait_ge(hidden, now.done(C, c + 1))
                            wait(act, act_lo_ready, now.done(C, c - 1))
                            nc.scalar.activation(act32[:, c % 2, :], ps_h[c % 2][:, :], ACT.Gelu, bias=b1_f[:, now.p, c:c + 1],
                                                 scale=1.0 / (SA * SW)).then_inc(act_ready, 1)
                            act.wait_ge(act_ready, now.done(C, c + 1))
                            wait(act, second, now.done(C, c - 3))
                            nc.scalar.activation(act_hi[:, c % 4, :], act32[:, c % 2, :], ACT.Copy, scale=SA).then_inc(act_hi_ready, 1)
                        if c == 2 and s.there():
                            if s.p == 0:
                                act.wait_ge(in_ready, s.group() + 1)
                            else:
                                act.wait_ge(x_ready, Unit(T, j - 2, G).done(1, 1))
                            wait(act, mixed, s.done(2))
                            nc.scalar.activation(x_hi[:, :, :], xs[s.p][:, :, :], ACT.Copy, scale=SA).then_inc(x_hi_ready, 1)
                        if c == 4 and s.there():
                            act.wait_ge(shift_ready, s.done(1, 1))
                            wait(act, p_lo_ready, s.done(2))
                            nc.scalar.activation(expd[:, :, :], shifted[:, :, :], ACT.Exp).then_inc(exp_ready, 1)
                        if c == 5 and w.there():
                            act.wait_ge(h_ready, w.done(R, R))
                            wait(act, h_turned, w.done(2))
                            nc.scalar.activation(h_hi[:, :, :], h[:, :, :], ACT.Copy, scale=SA).then_inc(h_hi_ready, 1)
                        if c == 6 and j == 0 and e is not None:
                            act.wait_ge(in_norm, e * R + R)
                            wait(act, u_ready, Unit(T, j + 3, G).done(R, R, before=1))
                            nc.scalar.activation(xs[0][:, :, :], x_in[:, :, :], ACT.Relu).then_inc(in_ready, 1)
                        if c == 7 and s.there():
                            act.wait_ge(p_turned, s.done(1, 1))
                            nc.scalar.activation(pt[:, :, :, :].rearrange("p s r i -> p (s r i)"), ps_t[:, :],
                                                 ACT.Copy).then_inc(pt_ready, 1)
                        if c == 7 and w.there():
                            act.wait_ge(h_turned, w.done(2, 1))
                            nc.scalar.activation(ht[w.p][:, 0, :, :], ps_s[:, :, :], ACT.Copy).then_inc(ht_ready, 1)
                            act.wait_ge(h_turned, w.done(2, 2))
                            nc.scalar.activation(ht[w.p][:, 1, :, :].rearrange("p k r -> p (k r)"), ps_t[:, :],
                                                 ACT.Copy).then_inc(ht_ready, 1)
                        if g is None or j != 1:
                            continue
                        if c == 3:
                            act.wait_ge(counted, g + 1)
                            nc.scalar.activation(counts[:, :], ps_s32[0:LABELS, :], ACT.Copy, scale=SL).then_inc(counts_ready, 1)
                            act.wait_ge(last_norm, g * R + R)
                            wait(act, r_turned, g * 2)
                            nc.scalar.activation(r_hi[:, :, :], last_n[:, :, :], ACT.Relu).then_inc(r_hi_ready, 1)
                        if c == 6:
                            act.wait_ge(r_turned, g * 2 + 1)
                            nc.scalar.activation(rt[:, 0, :, :], ps_s[:, :, :], ACT.Copy).then_inc(rt_ready, 1)
                            act.wait_ge(r_turned, g * 2 + 2)
                            nc.scalar.activation(rt[:, 1, :, :].rearrange("p k r -> p (k r)"), ps_t[:, :],
                                                 ACT.Copy).then_inc(rt_ready, 1)

            program(act, body)

        @block.vector
        def _(dve):
            dve.wait_ge(masks, 1)
            for s in range(2):
                rows = slice(s * N, (s + 1) * N)
                nc.vector.memset(blocks[rows, rows], 1.0)
                for l in range(LABELS // 2):
                    label = l + s * (LABELS // 2)
                    nc.vector.memset(labels[rows, l:l + 1], float(label))
                    set_last = nc.vector.memset(pick[rows, l, label:label + 1], 1.0)
            set_last.then_inc(halves_set, 1)

            def prepare(l):
                for k in range(K):
                    dve.wait_ge(w1_hi_ready, K * l + k + 1)
                    nc.vector.scalar_tensor_tensor(out=w1_lo[:, l, k, :], in0=stage1[:, k, :], scalar=g1_s[:, l, k:k + 1],
                                                   in1=w1_hi[:, l, k, :], op0=ALU.mult, op1=ALU.subtract).then_inc(w1_lo_ready, 1)
                dve.wait_ge(b1_summed, l + 1)
                nc.vector.tensor_tensor(b1_f[:, l, :], ps_f[0][:, 0, 0:C], b1_c[:, l, :], ALU.add).then_inc(b1_ready, 1)
                dve.wait_ge(w2_hi_ready, l + 1)
                nc.vector.scalar_tensor_tensor(out=w2_lo[:, l, :, :], in0=stage2[:, :, :], scalar=SW, in1=w2_hi[:, l, :, :],
                                               op0=ALU.mult, op1=ALU.subtract).then_inc(w2_lo_ready, 1)

            def prepare_last():
                dve.wait_ge(stage2_in, 16 * (L + 1))
                both = stage2[:, 0:2 * K, :].rearrange("p (k s) o -> p k s o", s=2)
                for s in range(2):
                    wait(dve, wl_steps, s)
                    nc.vector.tensor_tensor(wl_eye[:, :, :], wl_eye[:, :, :], both[:, :, s, :], ALU.add).then_inc(wl_steps, 1)
                dve.wait_ge(wl_hi_ready, 2)
                nc.vector.scalar_tensor_tensor(out=wl_lo[:, :, :], in0=wl_eye[:, :, :], scalar=SL, in1=wl_hi[:, :, :],
                                               op0=ALU.mult, op1=ALU.subtract).then_inc(wl_ready, 1)
                nc.vector.scalar_tensor_tensor(out=lab_lo[:, :], in0=lab_f[:, :], scalar=SL, in1=lab_hi[:, :],
                                               op0=ALU.mult, op1=ALU.subtract).then_inc(wl_ready, 1)

            def statistics(ln, of, done):
                for r in range(R):
                    nc.vector.bn_stats(stats[:, ln, r, :], of[:, r, :]).then_inc(done, 1)

            def aggregate(ln, mv_done, mv_value, var_done, scale=1.0):
                for r in range(R):
                    nc.vector.bn_aggr(mv[:, ln, r, :], stats[:, ln, r, :]).then_inc(mv_done, 1)
                dve.wait_ge(mv_done, mv_value)
                nc.vector.tensor_scalar(var[:, ln, :], mv[:, ln, :, 1], EPS, scale, ALU.add, ALU.mult).then_inc(var_done, 1)

            def normalize(ln, to, of, done):
                for r in range(R):
                    nc.vector.tensor_scalar(to[:, r, :], of[:, r, :], mv[:, ln, r, 0:1], rstd[:, ln, r:r + 1],
                                            ALU.subtract, ALU.mult).then_inc(done, 1)

            def body(T):
                e, g = entry(T), last(T)
                for j in range(L):
                    v, now, w, s, d = (Unit(T, j + i, G) for i in range(-1, 4))
                    if isinstance(T, int) and T == FIRST_T:
                        if j == 0:
                            dve.wait_ge(halves_set, 1)
                            dve.wait_ge(masks, MASK_STEPS)
                            dve.wait_ge(consts_in, 16 * CONSTS)
                            nc.vector.tensor_scalar(g1_s[:, :, :], g1_c[:, :, :], SW, None, ALU.mult).then_inc(g1s_ready, 1)
                            dve.wait_ge(g1s_ready, 1)
                        prepare(j)
                    if isinstance(T, int) and T == LAST_PREP_T and j == L - 1:
                        prepare_last()
                    for c in range(C):
                        if c == 0 and v.there():
                            dve.wait_ge(hb_ready, v.done(1, 1))
                            dve.wait_ge(second, v.done(C, C))
                            for i in range(2):
                                nc.vector.scalar_tensor_tensor(out=y[:, 2 * i:2 * i + 2, :], in0=ps_f[i][:, :, :], scalar=1.0 / (SA * SW),
                                                               in1=hb[v.p][:, 2 * i:2 * i + 2, :], op0=ALU.mult,
                                                               op1=ALU.add).then_inc(y_ready, 1)
                            dve.wait_ge(y_ready, v.done(2, 2))
                            statistics(LN_Y, y, y_stats)
                        if c == 1 and w.there():
                            for r in range(R):
                                if r % 2 == 0:
                                    dve.wait_ge(mixed, w.done(2, r // 2 + 1))
                                nc.vector.scalar_tensor_tensor(out=u[:, r, :], in0=ps_a[r // 2][:, r % 2, :],
                                                               scalar=inv_sum[:, w.p, r:r + 1], in1=xs[w.p][:, r, :],
                                                               op0=ALU.mult, op1=ALU.add).then_inc(u_ready, 1)
                        if c == 2 and w.there():
                            dve.wait_ge(u_ready, w.done(R, R))
                            statistics(LN_U, u, u_stats)
                        if c == 2 and j == 0 and e is not None:
                            dve.wait_ge(adj_loaded, e * 16 + 16)
                            nc.vector.tensor_tensor(adj_f[:, :, :], adj_in[:, :, :], delta[:, :].unsqueeze(1).to_broadcast([P, R, N]),
                                                    ALU.add).then_inc(adj_f_ready, 1)
                            dve.wait_ge(adj_f_ready, e + 1)
                            nc.vector.tensor_scalar(off[0][:, :, :], adj_f[:, :, :], 0.0, MASKED, ALU.is_le, ALU.mult).then_inc(off_ready[0], 1)
                            dve.wait_ge(x_loaded, e * 16 + 16)
                            statistics(LN_IN, x_in, in_stats)
                        if c == 3 and s.there():
                            dve.wait_ge(spread, s.done(1, 1))
                            mask = OFF_OF[s.p]
                            dve.wait_ge(off_ready[mask], s.group() + 1)
                            for r in range(R):
                                nc.vector.scalar_tensor_tensor(out=score[:, r, :], in0=ps_s32[:, r * N:(r + 1) * N],
                                                               scalar=s_ij[:, s.p, 0, r:r + 1], in1=off[mask][:, r, :],
                                                               op0=ALU.add, op1=ALU.add).then_inc(scored, 1)
                            dve.wait_ge(scored, s.done(R, R))
                            nc.vector.scalar_tensor_tensor(out=leaky[:, :, :], in0=score[:, :, :], scalar=SLOPE, in1=score[:, :, :],
                                                           op0=ALU.mult, op1=ALU.max).then_inc(leaked, 1)
                            dve.wait_ge(leaked, s.done(1, 1))
                            nc.vector.tensor_reduce(row_max[:, :], leaky[:, :, :], AX_X, ALU.max).then_inc(max_ready, 1)
                            dve.wait_ge(max_ready, s.done(1, 1))
                            nc.vector.tensor_tensor(shifted[:, :, :], leaky[:, :, :], row_max[:, :].unsqueeze(2).to_broadcast([P, R, N]),
                                                    ALU.subtract).then_inc(shift_ready, 1)
                        move = L + 4 - c
                        if j == L - 1 and 1 <= move <= L and more(T, T + 2 - move):
                            if move < L and more(T, T + 1 - move):
                                dve.wait_ge(off_ready[move + 1], T + 2 - move)
                            dve.wait_ge(off_ready[move - 1], T + 3 - move)
                            nc.vector.tensor_copy(off[move][:, :, :], off[move - 1][:, :, :]).then_inc(off_ready[move], 1)
                        if c == 4 and v.there():
                            dve.wait_ge(y_rstd, v.done(1, 1))
                            wait(dve, xg_ready, v.done(1))
                            normalize(LN_Y, xn, y, xn_ready)
                        if c == 4 and w.there():
                            dve.wait_ge(u_rstd, w.done(1, 1))
                            wait(dve, hg_ready, w.done(1))
                            normalize(LN_U, h, u, h_ready)
                        if c == 4 and j == 0 and e is not None:
                            dve.wait_ge(in_rstd, e + 1)
                            normalize(LN_IN, x_in, x_in, in_norm)
                        if c == 5 and s.there():
                            dve.wait_ge(exp_ready, s.done(1, 1))
                            wait(dve, p_turned, s.done(1))
                            nc.vector.tensor_reduce(row_sum[:, :], expd[:, :, :], AX_X, ALU.add).then_inc(sum_ready, 1)
                            for i in range(2):
                                rows = slice(i * N, (i + 1) * N)
                                nc.vector.tensor_scalar(p_hi[rows, :, rows], expd[rows, :, :], SP, None, ALU.mult).then_inc(p_hi_ready, 1)
                            for i in range(2):
                                rows = slice(i * N, (i + 1) * N)
                                dve.wait_ge(p_hi_ready, s.done(2, i + 1))
                                nc.vector.scalar_tensor_tensor(out=p_lo[rows, :, rows], in0=expd[rows, :, :], scalar=SP,
                                                               in1=p_hi[rows, :, rows], op0=ALU.mult,
                                                               op1=ALU.subtract).then_inc(p_lo_ready, 1)
                            dve.wait_ge(sum_ready, s.done(1, 1))
                            nc.vector.tensor_scalar(row_sum_s[:, :], row_sum[:, :], SP * SA, None, ALU.mult).then_inc(sum_scaled, 1)
                            dve.wait_ge(sum_scaled, s.done(1, 1))
                            nc.vector.reciprocal(inv_sum[:, s.p, :], row_sum_s[:, :]).then_inc(inv_ready, 1)
                        if c == 6 and w.there():
                            dve.wait_ge(h_hi_ready, w.done(1, 1))
                            nc.vector.scalar_tensor_tensor(out=h_lo[:, :, :], in0=h[:, :, :], scalar=SA, in1=h_hi[:, :, :],
                                                           op0=ALU.mult, op1=ALU.subtract).then_inc(h_lo_ready, 1)
                        if c == 6 and s.there():
                            dve.wait_ge(x_hi_ready, s.done(1, 1))
                            nc.vector.scalar_tensor_tensor(out=x_lo[:, :, :], in0=xs[s.p][:, :, :], scalar=SA, in1=x_hi[:, :, :],
                                                           op0=ALU.mult, op1=ALU.subtract).then_inc(x_lo_ready, 1)
                        if j == 1 and c == 0 and g is not None:
                            dve.wait_ge(adjt_loaded, g * 32 + 32)
                            nc.vector.tensor_copy(adjt_h[:, :], adjt_in[:, :]).then_inc(adjt_h_ready, 1)
                            dve.wait_ge(adjt_h_ready, g + 1)
                            wait(dve, counted, g)
                            for l in range(LABELS // 2):
                                one = nc.vector.tensor_scalar(onehot[:, l, :], adjt_h[:, :], labels[:, l:l + 1], None, ALU.is_equal)
                            one.then_inc(onehot_ready, 1)
                            dve.wait_ge(x2_ready, g + 1)
                            statistics(LN_LAST, x2, last_stats)
                        tail_step, mix_step = c == 0 and v.there(), c == 2 and w.there()
                        last_step, entry_step = c == 0 and j == 1 and g is not None, c == 2 and j == 0 and e is not None
                        if tail_step:
                            dve.wait_ge(y_stats, v.done(R, R))
                        if mix_step:
                            dve.wait_ge(u_stats, w.done(R, R))
                        if last_step:
                            dve.wait_ge(last_stats, g * R + R)
                        if entry_step:
                            dve.wait_ge(in_stats, e * R + R)
                        if now.there():
                            dve.wait_ge(act_hi_ready, now.done(C, c + 1))
                            nc.vector.scalar_tensor_tensor(out=act_lo[:, c % 4, :], in0=act32[:, c % 2, :], scalar=SA,
                                                           in1=act_hi[:, c % 4, :], op0=ALU.mult,
                                                           op1=ALU.subtract).then_inc(act_lo_ready, 1)
                        if tail_step:
                            aggregate(LN_Y, y_mv, v.done(R, R), y_var)
                        if mix_step:
                            aggregate(LN_U, u_mv, w.done(R, R), u_var)
                        if last_step:
                            aggregate(LN_LAST, last_mv, g * R + R, last_var, scale=SL ** -2)
                        if entry_step:
                            aggregate(LN_IN, in_mv, e * R + R, in_var)
                        if c == 7 and d.there():
                            if d.p == 0:
                                dve.wait_ge(in_ready, d.group() + 1)
                            else:
                                dve.wait_ge(x_ready, v.done(1, 1))
                            for r in range(R):
                                for i in range(2):
                                    wait(dve, dots_ready, d.done(2 * R, 2 * r + i - 1))
                                    nc.vector.tensor_tensor_reduce(dots_junk[:, i, :], xs[d.p][:, r, :], attn_r[:, d.p, i, :], 1.0,
                                                                   attn_b_r[:, d.p:d.p + 1] if i == 0 else 0.0, ALU.mult, ALU.add,
                                                                   s_ij[:, d.p, i, r:r + 1]).then_inc(dots_ready, 1)
                            dve.wait_ge(dots_ready, d.done(2 * R, 2 * R))
                            wait(dve, spread, d.done(1))
                            nc.vector.tensor_tensor(diag[:, :, :], delta[:, :].unsqueeze(1).to_broadcast([P, R, N]),
                                                    s_ij[:, d.p, 1, :].unsqueeze(2).to_broadcast([P, R, N]), ALU.mult).then_inc(diag_ready, 1)
                        if g is None:
                            continue
                        if j == 1 and c == 2:
                            dve.wait_ge(last_rstd, g + 1)
                            normalize(LN_LAST, last_n, x2, last_norm)
                        if j == 1 and c == 4:
                            dve.wait_ge(r_hi_ready, g + 1)
                            wait(dve, r_turned, g * 2)
                            nc.vector.scalar_tensor_tensor(out=r_lo[:, :, :], in0=last_n[:, :, :], scalar=0.0, in1=r_hi[:, :, :],
                                                           op0=ALU.max, op1=ALU.subtract).then_inc(r_lo_ready, 1)
                        if j == 2 and c == 3:
                            wait(dve, stored, g * 16)
                            for i in range(2):
                                dve.wait_ge(mapped, g * 2 + i + 1)
                                nc.vector.scalar_tensor_tensor(out=result[:, 2 * i:2 * i + 2, :], in0=ps_a[i][:, :, :],
                                                               scalar=1.0 / (SL * SL), in1=x2[:, 2 * i:2 * i + 2, :],
                                                               op0=ALU.mult, op1=ALU.add).then_inc(result_ready, 1)

            program(dve, body)

        @block.tensor
        def _(pe):
            def prepare(l):
                pe.wait_ge(consts_in, 16 * CONSTS)
                pe.wait_ge(stage1_in, 16 * (l + 1))
                wait(pe, b1_ready, l)
                for c in range(C):
                    for k in range(K):
                        mm = nc.tensor.matmul(ps_f[0][:, 0, c:c + 1], stage1[:, k, c * P:(c + 1) * P], beta1_c[:, l, k:k + 1],
                                              start=(k == 0), stop=(k == K - 1))
                mm.then_inc(b1_summed, 1)

            def first_product(v, c):
                for k in range(K):
                    for n, (a, b) in enumerate(((w1_hi, 0), (w1_hi, 1), (w1_lo, 0))):
                        mm = nc.tensor.matmul(ps_h[c % 2][:, :], a[:, v.p, k, c * P:(c + 1) * P], ht[v.p][:, b, k, :],
                                              start=(k == 0 and n == 0), stop=(k == K - 1 and n == 2))
                mm.then_inc(hidden, 1)

            def second_product(v, c):
                pe.wait_ge(act_lo_ready, v.done(C, c + 1))
                if c == 0:
                    wait(pe, y_ready, v.done(2))
                for r in range(R):
                    for n, (a, b) in enumerate(((act_hi, w2_hi), (act_hi, w2_lo), (act_lo, w2_hi))):
                        mm = nc.tensor.matmul(ps_f[r // 2][:, r % 2, :], a[:, c % 4, r * P:(r + 1) * P], b[:, v.p, c, :],
                                              start=(c == 0 and r % 2 == 0 and n == 0), stop=(c == C - 1 and n == 2),
                                              skip_group_check=True)
                mm.then_inc(second, 1)

            def turn(to_hi, hi, to_lo, lo, done):
                for to, of in ((to_hi, hi), (to_lo, lo)):
                    for r in range(R):
                        for k in range(K):
                            mm = nc.tensor.transpose(to[:, k, r * P:(r + 1) * P], of[:, r, k * P:(k + 1) * P], ident[:, :])
                    mm.then_inc(done, 1)

            ps_t_k = ps_t[:, :].rearrange("p (k r) -> p k r", k=K)
            pe.wait_ge(masks, MASK_STEPS)
            pe.wait_ge(halves_set, 1)

            def body(T):
                g = last(T)
                for j in range(L):
                    now, w, s = Unit(T, j, G), Unit(T, j + 1, G), Unit(T, j + 2, G)
                    if isinstance(T, int) and T == FIRST_T:
                        prepare(j)
                    for c in range(C):
                        if now.there():
                            if c == 0:
                                pe.wait_ge(ht_ready, now.done(2, 2))
                                if now.fixed:
                                    pe.wait_ge(w1_lo_ready, K * L)
                                    pe.wait_ge(w2_lo_ready, L)
                                    pe.wait_ge(b1_ready, L)
                            wait(pe, act_ready, now.done(C, c - 1))
                            first_product(now, c)
                            if c >= FFN_LAG:
                                second_product(now, c - FFN_LAG)
                        if c == 0 and w.there():
                            pe.wait_ge(pt_ready, w.done(1, 1))
                            pe.wait_ge(x_lo_ready, w.done(1, 1))
                            wait(pe, u_ready, w.done(R))
                            if j == 0:
                                results = groups_before(T - L)
                                wait(pe, result_ready, results * 2)
                            for r in range(R):
                                for n, (a, b) in enumerate(((0, x_hi), (0, x_lo), (1, x_hi))):
                                    mm = nc.tensor.matmul(ps_a[r // 2][:, r % 2, :], pt[:, a, r, :], b[:, r, :],
                                                          start=(n == 0), stop=(n == 2))
                                if r % 2:
                                    mm.then_inc(mixed, 1)
                        if c == 1 and s.there():
                            pe.wait_ge(diag_ready, s.done(1, 1))
                            wait(pe, ht_ready, w.done(2))
                            nc.tensor.matmul(ps_s32[:, 0:R * N], blocks[:, :], diag[:, :, :].rearrange("p r n -> p (r n)"),
                                             start=True, stop=True).then_inc(spread, 1)
                        if c == 2 and j == 1 and g is not None:
                            pe.wait_ge(onehot_ready, g + 1)
                            wait(pe, scored, upto(s, R))
                            wait(pe, ht_ready, upto(now, 2))
                            for l in range(LABELS // 2):
                                mm = nc.tensor.matmul(ps_s32[0:LABELS, :], pick[:, l, :], onehot[:, l, :],
                                                      start=(l == 0), stop=(l == LABELS // 2 - 1))
                            mm.then_inc(counted, 1)
                        if c == 5 and j == 1 and g is not None:
                            pe.wait_ge(r_lo_ready, g + 1)
                            pe.wait_ge(counts_ready, g + 1)
                            turn(ps_s, r_hi, ps_t_k, r_lo, r_turned)
                        if c == 6 and s.there():
                            pe.wait_ge(p_lo_ready, s.done(2, 2))
                            wait(pe, ht_ready, w.done(2))
                            if j == 1 and g is not None:
                                pe.wait_ge(rt_ready, g * 2 + 2)
                            for i, of in enumerate((p_hi, p_lo)):
                                for r in range(R):
                                    mm = nc.tensor.transpose(ps_t[:, (i * R + r) * P:(i * R + r + 1) * P], of[:, r, :], ident[:, :])
                            mm.then_inc(p_turned, 1)
                        if c == 7 and w.there():
                            pe.wait_ge(h_lo_ready, w.done(1, 1))
                            wait(pe, scored, upto(s, R))
                            wait(pe, pt_ready, upto(s, 1))
                            if j == 1 and g is not None:
                                pe.wait_ge(rt_ready, g * 2 + 2)
                            turn(ps_s, h_hi, ps_t_k, h_lo, h_turned)
                        if c == 2 and j == 2 and g is not None:
                            pe.wait_ge(rt_ready, g * 2 + 2)
                            pe.wait_ge(wl_ready, 2)
                            wait(pe, u_ready, upto(w, R))
                            for r in range(R):
                                tile = slice(r * P, (r + 1) * P)
                                for n, (a, b) in enumerate(((0, wl_hi), (0, wl_lo), (1, wl_hi))):
                                    for k in range(K):
                                        nc.tensor.matmul(ps_a[r // 2][:, r % 2, :], rt[:, a, k, tile], b[:, k, :],
                                                         start=(n == 0 and k == 0), stop=False)
                                nc.tensor.matmul(ps_a[r // 2][:, r % 2, :], counts[:, tile], lab_hi[:, :], start=False, stop=False)
                                mm = nc.tensor.matmul(ps_a[r // 2][:, r % 2, :], counts[:, tile], lab_lo[:, :], start=False, stop=True)
                                if r % 2:
                                    mm.then_inc(mapped, 1)
                    if now.there():
                        for c in range(C - FFN_LAG, C):
                            second_product(now, c)

            program(pe, body)


def kernel(x, adj, L0_gnn_attn_w, L0_gnn_attn_b, L0_gnn_W1, L0_gnn_b1, L0_gnn_W2, L0_gnn_b2, L0_gnn_g1, L0_gnn_beta1,
           L0_gnn_g2, L0_gnn_beta2, L1_gnn_weights, L1_gnn_bias):
    import concourse.bacc as bacc
    import numpy as np
    from concourse.bass_utils import run_bass_kernel_spmd

    x, adj = np.asarray(x), np.asarray(adj)
    graphs = P // N * R

    def by_partition(a):
        a = np.asarray(a)
        return a.reshape(a.shape[0], -1, P).transpose(2, 0, 1)

    def row(a):
        return np.asarray(a).reshape(1, -1)

    arrays = {
        "x": x.reshape(-1, D),
        "adj": adj.reshape(-1, N),
        "adj_t": adj.reshape(-1, graphs, N, N).transpose(0, 3, 1, 2).reshape(-1, N, ROWS),
        "attn_w": row(L0_gnn_attn_w),
        "attn_b": row(L0_gnn_attn_b),
        "w1": L0_gnn_W1,
        "b1": by_partition(L0_gnn_b1),
        "w2": L0_gnn_W2,
        "b2": row(L0_gnn_b2),
        "g1": by_partition(L0_gnn_g1),
        "g1_row": row(L0_gnn_g1),
        "beta1": by_partition(L0_gnn_beta1),
        "beta1_row": row(L0_gnn_beta1),
        "g2": row(L0_gnn_g2),
        "beta2": row(L0_gnn_beta2),
        "wl": np.asarray(L1_gnn_weights).transpose(2, 0, 1).reshape(K, P, -1, D).transpose(1, 0, 2, 3).reshape(P, -1, D),
        "lab": L1_gnn_bias,
    }
    arrays = {f"in_{n}": np.ascontiguousarray(a) for n, a in arrays.items()}
    nc = bacc.Bacc("TRN2", target_bir_lowering=False, num_devices=1)
    args = [nc.dram_tensor(n, a.shape, mybir.dt.from_np(a.dtype), kind="ExternalInput").ap() for n, a in arrays.items()]
    out = nc.dram_tensor("out", arrays["in_x"].shape, F32, kind="ExternalOutput").ap()
    gnn_block(nc, *args, out)
    got = run_bass_kernel_spmd(nc, [arrays], core_ids=[0]).results[0]["out"]
    return got.reshape(x.shape)
```

```python
from contextlib import ExitStack

import concourse.bass as bass
from concourse import mybir

F32 = mybir.dt.float32
F16 = mybir.dt.float16
I32 = mybir.dt.int32
ALU = mybir.AluOpType
ACT = mybir.ActivationFunctionType
AX_X = mybir.AxisListType.X

P = 128
N = 64
D = 256
K = D // P
F = 4 * D
C = F // P
L = 3
LABELS = 16
R = 4
ROWS = R * P
EPS = 1e-5
SLOPE = 0.2
RING = 4
TEAM = 4
TURN = L * TEAM
MASKED = -1e30
SA = 16.0
SP = 256.0
SW = 64.0
SL = 16.0
FFN_LAG = 3


class Unit:

    def __init__(self, B, j, units):
        self.B, self.j, self.units = B, j, units
        self.fixed = isinstance(B, int)
        self.p = j // TEAM % L

    def there(self):
        return not self.fixed or 0 <= self.B * TURN + self.j < self.units

    def group(self):
        return self.B * TEAM + (self.j // TURN * TEAM + self.j % TEAM)

    def turns_of_two(self):
        return self.B * (TEAM // 2) + ((self.j // TURN * TEAM + self.j % TEAM) // 2 + 1)

    def ends(self):
        return self.p == L - 1 and self.there()

    def starts(self):
        return self.p == 0 and self.there()

    def done(self, each, n=0):
        if not self.fixed:
            return self.B * (TURN * each) + (self.j * each + n)
        k = self.B * TURN + self.j
        return min(max(k, 0), self.units) * each + (n if self.there() else 0)


def gnn_block(nc, x, adj, adjt_g, attn_w, attn_b, w1, b1, w2, b2, g1, g1_row, beta1, beta1_row, g2, beta2, wl, lab, out):
    G = x.shape[0] // ROWS

    x_g = x.rearrange("(g r p) d -> g p r d", r=R, p=P)
    adj_g = adj.rearrange("(g r p) n -> g p r n", r=R, p=P)
    out_g = out.rearrange("(g r p) d -> g p r d", r=R, p=P)

    ctx = ExitStack()
    with ctx:
        def sb(name, shape, dt=F32):
            return ctx.enter_context(nc.sbuf_tensor(name, shape, dt))

        def psum(name, shape, dt=F32):
            return ctx.enter_context(nc.psum_tensor(name, shape, dt))

        def sem(name):
            return ctx.enter_context(nc.semaphore(name))

        w1_hi = sb("w1_hi", [P, L, K, F], F16)
        w1_lo = sb("w1_lo", [P, L, K, F], F16)
        w2_hi = sb("w2_hi", [P, L, C, D], F16)
        w2_lo = sb("w2_lo", [P, L, C, D], F16)
        wl_hi = sb("wl_hi", [P, K, D], F16)
        wl_lo = sb("wl_lo", [P, K, D], F16)
        lab_hi = sb("lab_hi", [LABELS, D], F16)
        lab_lo = sb("lab_lo", [LABELS, D], F16)
        stage1 = sb("stage1", [P, K, F])
        stage2 = sb("stage2", [P, C, D])
        lab_f = sb("lab_f", [LABELS, D])
        g1_r = sb("g1_r", [P, L, D])
        c1_r = sb("c1_r", [P, L, D])
        b2_r = sb("b2_r", [P, L, D])
        g2_r = sb("g2_r", [P, L, D])
        beta2_r = sb("beta2_r", [P, L, D])
        attn_r = sb("attn_r", [P, L, 2, D])
        attn_b_r = sb("attn_b_r", [P, L])
        g1_c = sb("g1_c", [P, L, K])
        g1_s = sb("g1_s", [P, L, K])
        beta1_c = sb("beta1_c", [P, L, K])
        b1_c = sb("b1_c", [P, L, C])
        b1_f = sb("b1_f", [P, L, C])
        ident = sb("ident", [P, P], F16)
        blocks = sb("blocks", [P, P])
        delta = sb("delta", [P, N])
        wl_eye = sb("wl_eye", [P, K, D])
        labels = sb("labels", [P, LABELS // 2])
        pick = sb("pick", [P, LABELS // 2, LABELS], F16)
        half = sb("half", [P, R])
        x_in = [sb(f"x_in{i}", [P, R, D]) for i in range(2)]
        x_again = sb("x_again", [P, R, D])
        adj_in = sb("adj_in", [P, R, N], I32)
        adjt_in = sb("adjt_in", [P, ROWS], I32)
        adj_f = sb("adj_f", [P, R, N])
        off = [sb(f"off{i}", [P, R, N]) for i in range(TEAM)]
        xs = [sb(f"xs{i}", [P, R, D]) for i in range(3)]
        x_hi = sb("x_hi", [P, R, D], F16)
        x_lo = sb("x_lo", [P, R, D], F16)
        s_ij = sb("s_ij", [P, 2, 2, R])
        dots_junk = sb("dots_junk", [P, 2, D])
        diag = sb("diag", [P, R, N])
        score = sb("score", [P, R, N])
        leaky = sb("leaky", [P, R, N])
        row_max = sb("row_max", [P, R])
        shifted = sb("shifted", [P, R, N])
        expd = sb("expd", [P, R, N])
        row_sum = sb("row_sum", [P, R])
        row_sum_s = sb("row_sum_s", [P, R])
        inv_sum = sb("inv_sum", [P, 2, R])
        p_hi = sb("p_hi", [P, R, P], F16)
        p_lo = sb("p_lo", [P, R, P], F16)
        pt = sb("pt", [P, 2, R, P], F16)
        u = sb("u", [P, R, D])
        h = u
        h_hi = sb("h_hi", [P, R, D], F16)
        h_lo = sb("h_lo", [P, R, D], F16)
        ht = [sb(f"ht{i}", [P, 2, K, ROWS], F16) for i in range(2)]
        hb = [sb(f"hb{i}", [P, R, D]) for i in range(2)]
        act32 = sb("act32", [P, RING, ROWS])
        act_hi = sb("act_hi", [P, RING, ROWS], F16)
        act_lo = sb("act_lo", [P, RING, ROWS], F16)
        y = sb("y", [P, R, D])
        xn = y
        LN_Y, LN_U, LN_IN, LN_LAST = range(4)
        stats = sb("stats", [P, 4, R, 6])
        mv = sb("mv", [P, 4, R, 2])
        var = sb("var", [P, 4, R])
        neg_mean = sb("neg_mean", [P, 4, R])
        rstd = sb("rstd", [P, 4, R])
        shift = sb("shift", [P, 4, R])
        x2 = [sb(f"x2_{i}", [P, R, D]) for i in range(2)]
        r_hi = sb("r_hi", [P, R, D], F16)
        r_lo = sb("r_lo", [P, R, D], F16)
        rt = sb("rt", [P, 2, K, ROWS], F16)
        adjt_h = sb("adjt_h", [P, ROWS], F16)
        onehot = stage2[:, :, :].bitcast(F16).rearrange("p l (s d) -> p (l s d)", s=2).rearrange("p (l r) -> p l r", r=ROWS)
        counts = sb("counts", [LABELS, ROWS], F16)
        last_n = stage1[:, 0, :].rearrange("p (r d) -> p r d", r=R)
        result = stage1[:, 1, :].rearrange("p (r d) -> p r d", r=R)

        ps_h = [psum(f"ps_h{i}", [P, ROWS]) for i in range(2)]
        ps_f = [psum(f"ps_f{i}", [P, 2, D]) for i in range(2)]
        ps_a = [psum(f"ps_a{i}", [P, 2, D]) for i in range(2)]
        ps_s = psum("ps_s", [P, K, ROWS], F16)
        ps_t = psum("ps_t", [P, 2 * ROWS], F16)
        ps_s32 = ps_s[:, :, :].rearrange("p k r -> p (k r)").bitcast(F32)
        ps_counts = ps_a[0][0:LABELS, :, :].rearrange("p s d -> p (s d)")

        consts_in = sem("consts_in")
        stage1_in = sem("stage1_in")
        stage2_in = sem("stage2_in")
        lab_in = sem("lab_in")
        x_loaded = [sem(f"x_loaded{i}") for i in range(2)]
        adj_loaded = sem("adj_loaded")
        x_again_loaded = sem("x_again_loaded")
        adjt_loaded = sem("adjt_loaded")
        stored = sem("stored")
        masks = sem("masks")
        halves_set = sem("halves_set")
        c1_ready = sem("c1_ready")
        rows_scaled = sem("rows_scaled")
        g1s_ready = sem("g1s_ready")
        w1_hi_ready = sem("w1_hi_ready")
        w1_lo_ready = sem("w1_lo_ready")
        w2_hi_ready = sem("w2_hi_ready")
        w2_lo_ready = sem("w2_lo_ready")
        b1_summed = sem("b1_summed")
        b1_ready = sem("b1_ready")
        wl_steps = sem("wl_steps")
        wl_hi_ready = sem("wl_hi_ready")
        wl_ready = sem("wl_ready")
        in_stats = sem("in_stats")
        in_mv = sem("in_mv")
        in_var = sem("in_var")
        in_rstd = sem("in_rstd")
        in_norm = sem("in_norm")
        in_ready = sem("in_ready")
        adj_f_ready = sem("adj_f_ready")
        off_ready = sem("off_ready")
        dots_ready = sem("dots_ready")
        diag_ready = sem("diag_ready")
        spread = sem("spread")
        scored = sem("scored")
        leaked = sem("leaked")
        max_ready = sem("max_ready")
        shift_ready = sem("shift_ready")
        exp_ready = sem("exp_ready")
        sum_ready = sem("sum_ready")
        sum_scaled = sem("sum_scaled")
        inv_ready = sem("inv_ready")
        p_hi_ready = sem("p_hi_ready")
        p_lo_ready = sem("p_lo_ready")
        p_turned = sem("p_turned")
        pt_ready = sem("pt_ready")
        x_hi_ready = sem("x_hi_ready")
        x_lo_ready = sem("x_lo_ready")
        mixed = sem("mixed")
        u_ready = sem("u_ready")
        u_stats = sem("u_stats")
        u_mv = sem("u_mv")
        u_var = sem("u_var")
        u_rstd = sem("u_rstd")
        h_ready = sem("h_ready")
        h_hi_ready = sem("h_hi_ready")
        h_lo_ready = sem("h_lo_ready")
        h_turned = sem("h_turned")
        ht_ready = sem("ht_ready")
        hg_ready = sem("hg_ready")
        hb_ready = sem("hb_ready")
        hidden = sem("hidden")
        act_ready = sem("act_ready")
        act_hi_ready = sem("act_hi_ready")
        act_lo_ready = sem("act_lo_ready")
        second = sem("second")
        y_ready = sem("y_ready")
        y_stats = sem("y_stats")
        y_mv = sem("y_mv")
        y_var = sem("y_var")
        y_rstd = sem("y_rstd")
        xn_ready = sem("xn_ready")
        xg_ready = sem("xg_ready")
        x_ready = sem("x_ready")
        x_again_ready = sem("x_again_ready")
        last_stats = sem("last_stats")
        last_mv = sem("last_mv")
        last_var = sem("last_var")
        last_rstd = sem("last_rstd")
        last_norm = sem("last_norm")
        r_hi_ready = sem("r_hi_ready")
        r_lo_ready = sem("r_lo_ready")
        r_turned = sem("r_turned")
        rt_ready = sem("rt_ready")
        adjt_h_ready = sem("adjt_h_ready")
        onehot_ready = sem("onehot_ready")
        counted = sem("counted")
        counts_ready = sem("counts_ready")
        mapped = sem("mapped")
        result_ready = sem("result_ready")

        MASK_STEPS = 6
        CONSTS = 10
        HALVES = (range(0, R // 2), range(R // 2, R))
        U = G * L
        BEFORE, AFTER = 3, 3

        def program(eng, body):
            for j in range(-BEFORE, TURN):
                body(0, j)
            with eng.Fori(1, G // TEAM - 1) as B:
                for j in range(TURN):
                    body(B, j)
            for j in range(TURN + AFTER):
                body(G // TEAM - 1, j)

        def upto(v, each):
            return v.done(each, each)

        block = ctx.enter_context(nc.Block())

        def wait(eng, semaphore, value):
            if not isinstance(value, int) or value > 0:
                eng.wait_ge(semaphore, value)

        @block.sync
        def _(sp):
            def load_constants():
                for tile, row in ((g1_c, g1), (beta1_c, beta1), (b1_c, b1)):
                    sp.dma_start(tile[:, :, :], row).then_inc(consts_in, 16)
                sp.dma_start(attn_r[:, :, :, :].rearrange("p l s d -> p (l s d)"), attn_w.to_broadcast([P, L * 2 * D])).then_inc(consts_in, 16)
                sp.dma_start(attn_b_r[:, :], attn_b.to_broadcast([P, L])).then_inc(consts_in, 16)
                for tile, row in ((g1_r, g1_row), (c1_r, beta1_row), (b2_r, b2), (g2_r, g2), (beta2_r, beta2)):
                    sp.dma_start(tile[:, :, :].rearrange("p l d -> p (l d)"), row.to_broadcast([P, L * D])).then_inc(consts_in, 16)

            def load_layer(l):
                wait(sp, w1_lo_ready, K * l)
                wait(sp, b1_summed, l)
                sp.dma_start(stage1[:, :, :], w1[l].rearrange("(k p) f -> p k f", p=P)).then_inc(stage1_in, 16)
                wait(sp, w2_lo_ready, l)
                sp.dma_start(stage2[:, :, :], w2[l].rearrange("(c p) d -> p c d", p=P)).then_inc(stage2_in, 16)

            def load_last_map():
                sp.wait_ge(w2_lo_ready, L)
                sp.dma_start(stage2[:, 0:2 * K, :], wl).then_inc(stage2_in, 16)
                sp.dma_start(lab_f[:, :], lab).then_inc(lab_in, 16)

            def body(B, j):
                coming, e, v, a3 = (Unit(B, j + i, U) for i in (4, 3, -1, -3))
                if j == -BEFORE:
                    sp.dma_start(x_in[e.j % 2][:, :, :], x_g[0]).then_inc(x_loaded[e.j % 2], 16)
                if coming.starts():
                    n = coming.group()
                    wait(sp, in_ready, (n - 1) * R)
                    sp.dma_start(x_in[coming.j % 2][:, :, :], x_g[n]).then_inc(x_loaded[coming.j % 2], 16)
                if e.starts():
                    n = e.group()
                    wait(sp, adj_f_ready, n)
                    sp.dma_start(adj_in[:, :, :], adj_g[n]).then_inc(adj_loaded, 16)
                if j == -BEFORE:
                    load_constants()
                if j < 0:
                    load_layer(j + BEFORE)
                if e.fixed and B == 0 and j == 0:
                    load_last_map()
                if v.ends():
                    n = v.group()
                    wait(sp, x_ready, Unit(B, j - 2, U).done(1, 1))
                    sp.dma_start(x_again[:, :, :], x_g[n]).then_inc(x_again_loaded, 16)
                    wait(sp, adjt_h_ready, n)
                    for s in range(2):
                        sp.dma_start(adjt_in[s * N:(s + 1) * N, :], adjt_g[n]).then_inc(adjt_loaded, 16)
                if a3.ends():
                    g = a3.group()
                    sp.wait_ge(result_ready, g * 2 + 2)
                    sp.dma_start(out_g[g], result[:, :, :]).then_inc(stored, 16)

            program(sp, body)
            sp.wait_ge(stored, 16 * G)

        @block.gpsimd
        def _(pool):
            def mark(view, pattern, base):
                return nc.gpsimd.affine_select(out=view, in_=view, compare_op=ALU.not_equal, fill=1.0, base=base,
                                               pattern=pattern, channel_multiplier=1)

            nc.gpsimd.memset(half[:, :], -0.5)
            nc.gpsimd.memset(delta[:, :], 0.0)
            nc.gpsimd.memset(ident[:, :], 0.0)
            nc.gpsimd.memset(wl_eye[:, :, :], 0.0)
            nc.gpsimd.memset(blocks[:, :], 0.0)
            nc.gpsimd.memset(pick[:, :, :], 0.0)
            nc.gpsimd.memset(p_hi[:, :, :], 0.0)
            nc.gpsimd.memset(p_lo[:, :, :], 0.0).then_inc(masks, 1)
            pool.wait_ge(masks, 1)
            mark(delta[:, :], [[-1, N]], 0).then_inc(masks, 1)
            pool.wait_ge(masks, 2)
            mark(delta[:, :], [[-1, N]], -N).then_inc(masks, 1)
            mark(ident[:, :], [[-1, P]], 0).then_inc(masks, 1)
            mark(wl_eye[:, 0, :], [[-1, D]], 0).then_inc(masks, 1)
            mark(wl_eye[:, 1, :], [[-1, D]], P).then_inc(masks, 1)
            pool.wait_ge(consts_in, 16 * CONSTS)
            nc.gpsimd.tensor_tensor(c1_r[:, :, :], c1_r[:, :, :], b2_r[:, :, :], ALU.add).then_inc(c1_ready, 1)
            pool.wait_ge(c1_ready, 1)
            pool.wait_ge(rows_scaled, 2)
            pool.wait_ge(masks, MASK_STEPS)

            def rows_of(tile, l):
                return tile[:, l, :].unsqueeze(1).to_broadcast([P, R, D])

            def scale_and_shift(ln, done, value):
                nc.gpsimd.tensor_tensor(rstd[:, ln, :], var[:, ln, :], half[:, :], ALU.pow).then_inc(done, 1)
                pool.wait_ge(done, value)
                nc.gpsimd.tensor_tensor(shift[:, ln, :], neg_mean[:, ln, :], rstd[:, ln, :], ALU.mult).then_inc(done, 1)

            def body(B, j):
                a2, v, now, w, e = (Unit(B, j + i, U) for i in (-2, -1, 0, 1, 3))
                if e.starts():
                    n = e.group()
                    pool.wait_ge(in_var, n * 2 + 2)
                    wait(pool, in_ready, n * R)
                    scale_and_shift(LN_IN, in_rstd, n * 2 + 1)
                if w.there():
                    pool.wait_ge(x_hi_ready, w.done(1, 1))
                    wait(pool, mixed, w.done(2))
                    nc.gpsimd.tensor_tensor(x_lo[:, :, :], xs[w.j % 3][:, :, :], x_hi[:, :, :], ALU.subtract).then_inc(x_lo_ready, 1)
                if v.ends():
                    g = v.group()
                    pool.wait_ge(x_again_loaded, g * 16 + 16)
                    nc.gpsimd.tensor_tensor(x_again[:, :, :], x_again[:, :, :], rows_of(beta2_r, L - 1), ALU.add).then_inc(x_again_ready, 1)
                if w.there():
                    pool.wait_ge(u_var, w.done(2, 2))
                    scale_and_shift(LN_U, u_rstd, w.done(2, 1))
                    pool.wait_ge(h_ready, w.done(R, R))
                    wait(pool, y_ready, upto(v, 2))
                    nc.gpsimd.tensor_tensor(hb[w.j % 2][:, :, :], h[:, :, :], rows_of(g1_r, w.p), ALU.mult).then_inc(hg_ready, 1)
                if v.there():
                    pool.wait_ge(y_var, v.done(2, 2))
                    scale_and_shift(LN_Y, y_rstd, v.done(2, 1))
                if w.there():
                    pool.wait_ge(hg_ready, w.done(1, 1))
                    nc.gpsimd.tensor_tensor(hb[w.j % 2][:, :, :], hb[w.j % 2][:, :, :], rows_of(c1_r, w.p), ALU.add).then_inc(hb_ready, 1)
                if a2.ends():
                    g = a2.group()
                    pool.wait_ge(last_var, g * 2 + 2)
                    scale_and_shift(LN_LAST, last_rstd, g * 2 + 1)
                if v.there():
                    pool.wait_ge(xn_ready, v.done(R, R))
                    if v.p < L - 1:
                        to, rest = xs[j % 3], rows_of(beta2_r, v.p)
                        wait(pool, u_ready, upto(now, R))
                    else:
                        to, rest = x2[v.j % 2], x_again[:, :, :]
                        wait(pool, result_ready, (v.group() - 1) * 2)
                    nc.gpsimd.tensor_tensor(to[:, :, :], xn[:, :, :], rows_of(g2_r, v.p), ALU.mult).then_inc(xg_ready, 1)
                    pool.wait_ge(xg_ready, v.done(1, 1))
                    if v.p == L - 1:
                        pool.wait_ge(x_again_ready, v.group() + 1)
                    nc.gpsimd.tensor_tensor(to[:, :, :], to[:, :, :], rest, ALU.add).then_inc(x_ready, 1)

            program(pool, body)

        @block.scalar
        def _(act):
            def prepare(l):
                act.wait_ge(g1s_ready, 1)
                act.wait_ge(stage1_in, 16 * (l + 1))
                for k in range(K):
                    nc.scalar.activation(w1_hi[:, l, k, :], stage1[:, k, :], ACT.Copy,
                                         scale=g1_s[:, l, k:k + 1]).then_inc(w1_hi_ready, 1)
                act.wait_ge(stage2_in, 16 * (l + 1))
                nc.scalar.activation(w2_hi[:, l, :, :], stage2[:, :, :], ACT.Copy, scale=SW).then_inc(w2_hi_ready, 1)

            def prepare_last():
                act.wait_ge(wl_steps, 2)
                nc.scalar.activation(wl_hi[:, :, :], wl_eye[:, :, :], ACT.Copy, scale=SL).then_inc(wl_hi_ready, 1)
                act.wait_ge(lab_in, 16)
                nc.scalar.activation(lab_hi[:, :], lab_f[:, :], ACT.Copy, scale=SL).then_inc(wl_hi_ready, 1)

            def body(B, j):
                a3, a2, v, now, w, s, e = (Unit(B, j + i, U) for i in (-3, -2, -1, 0, 1, 2, 3))
                if j < 0:
                    prepare(j + BEFORE)
                if now.fixed and B == 0 and j == 1:
                    prepare_last()
                for c in range(C):
                    if now.there():
                        if now.fixed and c == 0:
                            act.wait_ge(b1_ready, now.p + 1)
                        act.wait_ge(hidden, now.done(C, c + 1))
                        wait(act, act_lo_ready, now.done(C, c + 1 - RING))
                        nc.scalar.activation(act32[:, c % RING, :], ps_h[c % 2][:, :], ACT.Gelu, bias=b1_f[:, now.p, c:c + 1],
                                             scale=1.0 / (SA * SW)).then_inc(act_ready, 1)
                        act.wait_ge(act_ready, now.done(C, c + 1))
                        wait(act, second, now.done(2 * C, 2 * (c + 1 - RING)))
                        nc.scalar.activation(act_hi[:, c % RING, :], act32[:, c % RING, :], ACT.Copy, scale=SA).then_inc(act_hi_ready, 1)
                    if c == 0 and a3.ends():
                        g = a3.group()
                        act.wait_ge(counted, g + 1)
                        nc.scalar.activation(counts[:, :], ps_counts, ACT.Copy, scale=SL).then_inc(counts_ready, 1)
                    if c == 0 and w.there():
                        act.wait_ge(p_turned, w.done(1, 1))
                        wait(act, mixed, w.done(2))
                        nc.scalar.activation(pt[:, :, :, :].rearrange("p s r i -> p (s r i)"), ps_t[:, :],
                                             ACT.Copy).then_inc(pt_ready, 1)
                    if c == 1 and a3.ends():
                        g = a3.group()
                        act.wait_ge(r_turned, g * 2 + 1)
                        nc.scalar.activation(rt[:, 0, :, :], ps_s[:, :, :], ACT.Copy).then_inc(rt_ready, 1)
                        act.wait_ge(r_turned, g * 2 + 2)
                        nc.scalar.activation(rt[:, 1, :, :].rearrange("p k r -> p (k r)"), ps_t[:, :],
                                             ACT.Copy).then_inc(rt_ready, 1)
                    if c == 2 and s.there():
                        if s.p == 0:
                            act.wait_ge(in_ready, s.group() * R + R)
                        else:
                            act.wait_ge(x_ready, a2.done(1, 1))
                        wait(act, mixed, s.done(2))
                        nc.scalar.activation(x_hi[:, :, :], xs[s.j % 3][:, :, :], ACT.Copy).then_inc(x_hi_ready, 1)
                    if c == 3 and w.there():
                        act.wait_ge(u_rstd, w.done(2, 2))
                        for r in range(R):
                            nc.scalar.activation(h[:, r, :], u[:, r, :], ACT.Identity, bias=shift[:, LN_U, r:r + 1],
                                                 scale=rstd[:, LN_U, r:r + 1]).then_inc(h_ready, 1)
                    if c == 4 and s.there():
                        act.wait_ge(shift_ready, s.done(1, 1))
                        wait(act, p_lo_ready, s.done(2))
                        nc.scalar.activation(expd[:, :, :], shifted[:, :, :], ACT.Exp).then_inc(exp_ready, 1)
                    if c == 5 and v.there():
                        act.wait_ge(y_rstd, v.done(2, 2))
                        for r in range(R):
                            nc.scalar.activation(xn[:, r, :], y[:, r, :], ACT.Identity, bias=shift[:, LN_Y, r:r + 1],
                                                 scale=rstd[:, LN_Y, r:r + 1]).then_inc(xn_ready, 1)
                    if c == 6 and w.there():
                        act.wait_ge(h_turned, w.done(2, 1))
                        nc.scalar.activation(ht[w.j % 2][:, 0, :, :], ps_s[:, :, :], ACT.Copy).then_inc(ht_ready, 1)
                        act.wait_ge(h_turned, w.done(2, 2))
                        nc.scalar.activation(ht[w.j % 2][:, 1, :, :].rearrange("p k r -> p (k r)"), ps_t[:, :],
                                             ACT.Copy).then_inc(ht_ready, 1)
                    if c in (1, 2) and e.starts():
                        n = e.group()
                        act.wait_ge(in_rstd, n * 2 + 2)
                        wait(act, u_ready, upto(now, R))
                        for r in HALVES[c - 1]:
                            nc.scalar.activation(xs[j % 3][:, r, :], x_in[e.j % 2][:, r, :], ACT.Relu, bias=shift[:, LN_IN, r:r + 1],
                                                 scale=rstd[:, LN_IN, r:r + 1]).then_inc(in_ready, 1)
                    if c == 7 and a2.ends():
                        g = a2.group()
                        act.wait_ge(last_rstd, g * 2 + 2)
                        wait(act, r_lo_ready, g)
                        for r in range(R):
                            nc.scalar.activation(last_n[:, r, :], x2[a2.j % 2][:, r, :], ACT.Relu, bias=shift[:, LN_LAST, r:r + 1],
                                                 scale=rstd[:, LN_LAST, r:r + 1]).then_inc(last_norm, 1)

            program(act, body)

        @block.vector
        def _(dve):
            dve.wait_ge(masks, 1)
            for s in range(2):
                rows = slice(s * N, (s + 1) * N)
                nc.vector.memset(blocks[rows, rows], 1.0)
                for l in range(LABELS // 2):
                    label = l + s * (LABELS // 2)
                    nc.vector.memset(labels[rows, l:l + 1], float(label))
                    set_last = nc.vector.memset(pick[rows, l, label:label + 1], 1.0)
            set_last.then_inc(halves_set, 1)

            def prepare(l):
                for k in range(K):
                    dve.wait_ge(w1_hi_ready, K * l + k + 1)
                    nc.vector.scalar_tensor_tensor(out=w1_lo[:, l, k, :], in0=stage1[:, k, :], scalar=g1_s[:, l, k:k + 1],
                                                   in1=w1_hi[:, l, k, :], op0=ALU.mult, op1=ALU.subtract).then_inc(w1_lo_ready, 1)
                dve.wait_ge(b1_summed, l + 1)
                nc.vector.tensor_tensor(b1_f[:, l, :], ps_f[0][:, 0, 0:C], b1_c[:, l, :], ALU.add).then_inc(b1_ready, 1)
                dve.wait_ge(w2_hi_ready, l + 1)
                nc.vector.scalar_tensor_tensor(out=w2_lo[:, l, :, :], in0=stage2[:, :, :], scalar=SW, in1=w2_hi[:, l, :, :],
                                               op0=ALU.mult, op1=ALU.subtract).then_inc(w2_lo_ready, 1)

            def prepare_last():
                dve.wait_ge(stage2_in, 16 * (L + 1))
                both = stage2[:, 0:2 * K, :].rearrange("p (k s) o -> p k s o", s=2)
                for s in range(2):
                    wait(dve, wl_steps, s)
                    nc.vector.tensor_tensor(wl_eye[:, :, :], wl_eye[:, :, :], both[:, :, s, :], ALU.add).then_inc(wl_steps, 1)
                dve.wait_ge(wl_hi_ready, 2)
                nc.vector.scalar_tensor_tensor(out=wl_lo[:, :, :], in0=wl_eye[:, :, :], scalar=SL, in1=wl_hi[:, :, :],
                                               op0=ALU.mult, op1=ALU.subtract).then_inc(wl_ready, 1)
                nc.vector.scalar_tensor_tensor(out=lab_lo[:, :], in0=lab_f[:, :], scalar=SL, in1=lab_hi[:, :],
                                               op0=ALU.mult, op1=ALU.subtract).then_inc(wl_ready, 1)

            def statistics(ln, of, done):
                for r in range(R):
                    nc.vector.bn_stats(stats[:, ln, r, :], of[:, r, :]).then_inc(done, 1)

            def aggregate(ln, mv_done, mv_value, var_done, eps=EPS, scale=1.0):
                for r in range(R):
                    nc.vector.bn_aggr(mv[:, ln, r, :], stats[:, ln, r, :]).then_inc(mv_done, 1)
                dve.wait_ge(mv_done, mv_value)
                nc.vector.tensor_scalar(var[:, ln, :], mv[:, ln, :, 1], eps, scale, ALU.add, ALU.mult).then_inc(var_done, 1)
                nc.vector.tensor_scalar(neg_mean[:, ln, :], mv[:, ln, :, 0], -1.0, None, ALU.mult).then_inc(var_done, 1)

            def body(B, j):
                a3, a2, v, now, w, s, e = (Unit(B, j + i, U) for i in (-3, -2, -1, 0, 1, 2, 3))
                if j < 0:
                    if j == -BEFORE:
                        dve.wait_ge(halves_set, 1)
                        dve.wait_ge(masks, MASK_STEPS)
                        dve.wait_ge(consts_in, 16 * CONSTS)
                        nc.vector.tensor_scalar(g1_s[:, :, :], g1_c[:, :, :], SW, None, ALU.mult).then_inc(g1s_ready, 1)
                        dve.wait_ge(g1s_ready, 1)
                        for row in (g2_r, beta2_r):
                            nc.vector.tensor_scalar(row[:, 0:L - 1, :], row[:, 0:L - 1, :], SA, None, ALU.mult).then_inc(rows_scaled, 1)
                    prepare(j + BEFORE)
                if now.fixed and B == 0 and j == 1:
                    prepare_last()
                for c in range(C):
                    if c in (0, 1) and s.there():
                        if s.p == 0:
                            dve.wait_ge(in_ready, s.group() * R + R)
                        else:
                            dve.wait_ge(x_ready, a2.done(1, 1))
                        for r in HALVES[c]:
                            for i in range(2):
                                wait(dve, dots_ready, s.done(2 * R, 2 * r + i - 1))
                                nc.vector.tensor_tensor_reduce(dots_junk[:, i, :], xs[s.j % 3][:, r, :], attn_r[:, s.p, i, :], 1.0 / SA,
                                                               attn_b_r[:, s.p:s.p + 1] if i == 0 else 0.0, ALU.mult, ALU.add,
                                                               s_ij[:, s.j % 2, i, r:r + 1]).then_inc(dots_ready, 1)
                    if c == 1 and s.there():
                        dve.wait_ge(dots_ready, s.done(2 * R, 2 * R))
                        wait(dve, spread, s.done(1))
                        nc.vector.tensor_tensor(diag[:, :, :], delta[:, :].unsqueeze(1).to_broadcast([P, R, N]),
                                                s_ij[:, s.j % 2, 1, :].unsqueeze(2).to_broadcast([P, R, N]), ALU.mult).then_inc(diag_ready, 1)
                    if c == 0 and a3.ends():
                        g = a3.group()
                        dve.wait_ge(last_norm, g * R + R)
                        wait(dve, r_turned, g * 2)
                        nc.vector.tensor_copy(r_hi[:, :, :], last_n[:, :, :]).then_inc(r_hi_ready, 1)
                        dve.wait_ge(r_hi_ready, g + 1)
                        nc.vector.tensor_tensor(r_lo[:, :, :], last_n[:, :, :], r_hi[:, :, :], ALU.subtract).then_inc(r_lo_ready, 1)
                    mix_step = c == 2 and w.there()
                    if mix_step:
                        wait(dve, hg_ready, w.done(1))
                        dve.wait_ge(inv_ready, w.done(1, 1))
                        for r in range(R):
                            if r % 2 == 0:
                                dve.wait_ge(mixed, w.done(2, r // 2 + 1))
                            nc.vector.scalar_tensor_tensor(out=u[:, r, :], in0=ps_a[r // 2][:, r % 2, :],
                                                           scalar=inv_sum[:, w.j % 2, r:r + 1], in1=xs[w.j % 3][:, r, :],
                                                           op0=ALU.mult, op1=ALU.add).then_inc(u_ready, 1)
                        dve.wait_ge(u_ready, w.done(R, R))
                        statistics(LN_U, u, u_stats)
                    tail_step = c == 3 and v.there()
                    if tail_step:
                        dve.wait_ge(hb_ready, v.done(1, 1))
                        wait(dve, xg_ready, v.done(1))
                        for i in range(2):
                            dve.wait_ge(second, v.done(2 * C, 2 * C - 1 + i))
                            nc.vector.scalar_tensor_tensor(out=y[:, 2 * i:2 * i + 2, :], in0=ps_f[i][:, :, :], scalar=1.0 / (SA * SW),
                                                           in1=hb[v.j % 2][:, 2 * i:2 * i + 2, :], op0=ALU.mult,
                                                           op1=ALU.add).then_inc(y_ready, 1)
                    if c == 3 and s.there():
                        dve.wait_ge(spread, s.done(1, 1))
                        dve.wait_ge(off_ready, s.group() + 1)
                        for r in range(R):
                            nc.vector.scalar_tensor_tensor(out=score[:, r, :], in0=ps_s32[:, r * N:(r + 1) * N],
                                                           scalar=s_ij[:, s.j % 2, 0, r:r + 1], in1=off[s.j % TEAM][:, r, :],
                                                           op0=ALU.add, op1=ALU.add).then_inc(scored, 1)
                        dve.wait_ge(scored, s.done(R, R))
                        nc.vector.scalar_tensor_tensor(out=leaky[:, :, :], in0=score[:, :, :], scalar=SLOPE, in1=score[:, :, :],
                                                       op0=ALU.mult, op1=ALU.max).then_inc(leaked, 1)
                        dve.wait_ge(leaked, s.done(1, 1))
                        nc.vector.tensor_reduce(row_max[:, :], leaky[:, :, :], AX_X, ALU.max).then_inc(max_ready, 1)
                        dve.wait_ge(max_ready, s.done(1, 1))
                        nc.vector.tensor_tensor(shifted[:, :, :], leaky[:, :, :], row_max[:, :].unsqueeze(2).to_broadcast([P, R, N]),
                                                ALU.subtract).then_inc(shift_ready, 1)
                    if tail_step:
                        dve.wait_ge(y_ready, v.done(2, 2))
                        statistics(LN_Y, y, y_stats)
                    if c == 4 and w.there():
                        dve.wait_ge(h_ready, w.done(R, R))
                        wait(dve, h_turned, w.done(2))
                        nc.vector.tensor_scalar(h_hi[:, :, :], h[:, :, :], SA, None, ALU.mult).then_inc(h_hi_ready, 1)
                        dve.wait_ge(h_hi_ready, w.done(1, 1))
                        nc.vector.scalar_tensor_tensor(out=h_lo[:, :, :], in0=h[:, :, :], scalar=SA, in1=h_hi[:, :, :],
                                                       op0=ALU.mult, op1=ALU.subtract).then_inc(h_lo_ready, 1)
                    if c == 5 and e.starts():
                        n = e.group()
                        dve.wait_ge(adj_loaded, n * 16 + 16)
                        nc.vector.tensor_tensor(adj_f[:, :, :], adj_in[:, :, :], delta[:, :].unsqueeze(1).to_broadcast([P, R, N]),
                                                ALU.add).then_inc(adj_f_ready, 1)
                        dve.wait_ge(adj_f_ready, n + 1)
                        nc.vector.tensor_scalar(off[e.j % TEAM][:, :, :], adj_f[:, :, :], 0.0, MASKED, ALU.is_le, ALU.mult).then_inc(off_ready, 1)
                    last_step = c == 5 and a2.ends()
                    if last_step:
                        dve.wait_ge(x_ready, a2.done(1, 1))
                        statistics(LN_LAST, x2[a2.j % 2], last_stats)
                    if c in (5, 6) and a3.ends():
                        g = a3.group()
                        wait(dve, stored, g * 16)
                        i = c - 5
                        dve.wait_ge(mapped, g * 2 + i + 1)
                        nc.vector.scalar_tensor_tensor(out=result[:, 2 * i:2 * i + 2, :], in0=ps_a[i][:, :, :],
                                                       scalar=1.0 / (SL * SL), in1=x2[a3.j % 2][:, 2 * i:2 * i + 2, :],
                                                       op0=ALU.mult, op1=ALU.add).then_inc(result_ready, 1)
                    if c in (4, 7) and a2.ends():
                        g = a2.group()
                        if c == 4:
                            dve.wait_ge(adjt_loaded, g * 32 + 32)
                            nc.vector.tensor_copy(adjt_h[:, :], adjt_in[:, :]).then_inc(adjt_h_ready, 1)
                            dve.wait_ge(adjt_h_ready, g + 1)
                            wait(dve, counted, g)
                        for l in range(LABELS // 4) if c == 4 else range(LABELS // 4, LABELS // 2):
                            one = nc.vector.tensor_scalar(onehot[:, l, :], adjt_h[:, :], labels[:, l:l + 1], None, ALU.is_equal)
                        one.then_inc(onehot_ready, 1)
                    if c == 6 and s.there():
                        dve.wait_ge(exp_ready, s.done(1, 1))
                        wait(dve, p_turned, s.done(1))
                        nc.vector.tensor_reduce(row_sum[:, :], expd[:, :, :], AX_X, ALU.add).then_inc(sum_ready, 1)
                        for i in range(2):
                            rows = slice(i * N, (i + 1) * N)
                            nc.vector.tensor_scalar(p_hi[rows, :, rows], expd[rows, :, :], SP, None, ALU.mult).then_inc(p_hi_ready, 1)
                        for i in range(2):
                            rows = slice(i * N, (i + 1) * N)
                            dve.wait_ge(p_hi_ready, s.done(2, i + 1))
                            nc.vector.scalar_tensor_tensor(out=p_lo[rows, :, rows], in0=expd[rows, :, :], scalar=SP,
                                                           in1=p_hi[rows, :, rows], op0=ALU.mult,
                                                           op1=ALU.subtract).then_inc(p_lo_ready, 1)
                        dve.wait_ge(sum_ready, s.done(1, 1))
                        nc.vector.tensor_scalar(row_sum_s[:, :], row_sum[:, :], SP, None, ALU.mult).then_inc(sum_scaled, 1)
                        dve.wait_ge(sum_scaled, s.done(1, 1))
                        nc.vector.reciprocal(inv_sum[:, s.j % 2, :], row_sum_s[:, :]).then_inc(inv_ready, 1)
                    coming = Unit(B, j + 4, U) if c == 7 else e
                    entry_step = c == 7 and coming.starts() or j == -BEFORE and c == 0
                    if entry_step:
                        n = coming.group()
                        dve.wait_ge(x_loaded[coming.j % 2], coming.turns_of_two() * 16)
                        wait(dve, in_rstd, n * 2)
                        statistics(LN_IN, x_in[coming.j % 2], in_stats)
                    if tail_step:
                        dve.wait_ge(y_stats, v.done(R, R))
                    if mix_step:
                        dve.wait_ge(u_stats, w.done(R, R))
                    if last_step:
                        dve.wait_ge(last_stats, a2.group() * R + R)
                    if entry_step:
                        dve.wait_ge(in_stats, coming.group() * R + R)
                    of, chunk = (v, C - 1) if c == 0 else (now, c - 1)
                    if of.there():
                        dve.wait_ge(act_hi_ready, of.done(C, chunk + 1))
                        nc.vector.scalar_tensor_tensor(out=act_lo[:, chunk % RING, :], in0=act32[:, chunk % RING, :], scalar=SA,
                                                       in1=act_hi[:, chunk % RING, :], op0=ALU.mult,
                                                       op1=ALU.subtract).then_inc(act_lo_ready, 1)
                    if tail_step:
                        aggregate(LN_Y, y_mv, v.done(R, R), y_var)
                    if mix_step:
                        aggregate(LN_U, u_mv, w.done(R, R), u_var, eps=EPS * SA ** 2)
                    if last_step:
                        aggregate(LN_LAST, last_mv, a2.group() * R + R, last_var, scale=SL ** -2)
                    if entry_step:
                        aggregate(LN_IN, in_mv, coming.group() * R + R, in_var, scale=SA ** -2)

            program(dve, body)

        @block.tensor
        def _(pe):
            def prepare(l):
                pe.wait_ge(consts_in, 16 * CONSTS)
                pe.wait_ge(stage1_in, 16 * (l + 1))
                wait(pe, b1_ready, l)
                for c in range(C):
                    for k in range(K):
                        mm = nc.tensor.matmul(ps_f[0][:, 0, c:c + 1], stage1[:, k, c * P:(c + 1) * P], beta1_c[:, l, k:k + 1],
                                              start=(k == 0), stop=(k == K - 1))
                mm.then_inc(b1_summed, 1)

            def first_product(v, c):
                for k in range(K):
                    for n, (a, b) in enumerate(((w1_hi, 0), (w1_hi, 1), (w1_lo, 0))):
                        mm = nc.tensor.matmul(ps_h[c % 2][:, :], a[:, v.p, k, c * P:(c + 1) * P], ht[v.j % 2][:, b, k, :],
                                              start=(k == 0 and n == 0), stop=(k == K - 1 and n == 2))
                mm.then_inc(hidden, 1)

            def second_product(v, c):
                pe.wait_ge(act_lo_ready, v.done(C, c + 1))
                for r in range(R):
                    if c == 0 and r % 2 == 0:
                        wait(pe, y_ready, v.done(2, r // 2 - 1))
                    for n, (a, b) in enumerate(((act_hi, w2_hi), (act_hi, w2_lo), (act_lo, w2_hi))):
                        mm = nc.tensor.matmul(ps_f[r // 2][:, r % 2, :], a[:, c % RING, r * P:(r + 1) * P], b[:, v.p, c, :],
                                              start=(c == 0 and r % 2 == 0 and n == 0), stop=(c == C - 1 and n == 2),
                                              skip_group_check=True)
                    if r % 2:
                        mm.then_inc(second, 1)

            def turn(to_hi, hi, to_lo, lo, done):
                for to, of in ((to_hi, hi), (to_lo, lo)):
                    for r in range(R):
                        for k in range(K):
                            mm = nc.tensor.transpose(to[:, k, r * P:(r + 1) * P], of[:, r, k * P:(k + 1) * P], ident[:, :])
                    mm.then_inc(done, 1)

            ps_t_k = ps_t[:, :].rearrange("p (k r) -> p k r", k=K)
            pe.wait_ge(masks, MASK_STEPS)
            pe.wait_ge(halves_set, 1)

            def body(B, j):
                a3, a2, v, now, w, s, e = (Unit(B, j + i, U) for i in (-3, -2, -1, 0, 1, 2, 3))
                if j < 0:
                    prepare(j + BEFORE)
                for c in range(C):
                    if now.there():
                        if c == 0:
                            pe.wait_ge(ht_ready, now.done(2, 2))
                            if now.fixed and B == 0:
                                pe.wait_ge(w1_lo_ready, K * L)
                                pe.wait_ge(w2_lo_ready, L)
                                pe.wait_ge(b1_ready, L)
                        wait(pe, act_ready, now.done(C, c - 1))
                        first_product(now, c)
                    if c == 0 and w.there():
                        pe.wait_ge(p_lo_ready, w.done(2, 2))
                        wait(pe, ht_ready, upto(now, 2))
                        for i, of in enumerate((p_hi, p_lo)):
                            for r in range(R):
                                mm = nc.tensor.transpose(ps_t[:, (i * R + r) * P:(i * R + r + 1) * P], of[:, r, :], ident[:, :])
                        mm.then_inc(p_turned, 1)
                    if c == 1 and a3.ends():
                        g = a3.group()
                        pe.wait_ge(r_lo_ready, g + 1)
                        wait(pe, ht_ready, upto(now, 2))
                        wait(pe, pt_ready, upto(w, 1))
                        turn(ps_s, r_hi, ps_t_k, r_lo, r_turned)
                    if c == 1 and w.there():
                        pe.wait_ge(pt_ready, w.done(1, 1))
                        pe.wait_ge(x_lo_ready, w.done(1, 1))
                        wait(pe, u_ready, w.done(R))
                        a4 = Unit(B, j - 4, U)
                        if a4.ends():
                            pe.wait_ge(result_ready, a4.group() * 2 + 2)
                        if a3.ends():
                            pe.wait_ge(counts_ready, a3.group() + 1)
                        for r in range(R):
                            for n, (a, b) in enumerate(((0, x_hi), (0, x_lo), (1, x_hi))):
                                mm = nc.tensor.matmul(ps_a[r // 2][:, r % 2, :], pt[:, a, r, :], b[:, r, :],
                                                      start=(n == 0), stop=(n == 2))
                            if r % 2:
                                mm.then_inc(mixed, 1)
                    if c == 2 and s.there():
                        pe.wait_ge(diag_ready, s.done(1, 1))
                        wait(pe, ht_ready, upto(now, 2))
                        if a3.ends():
                            pe.wait_ge(rt_ready, a3.group() * 2 + 2)
                        nc.tensor.matmul(ps_s32[:, 0:R * N], blocks[:, :], diag[:, :, :].rearrange("p r n -> p (r n)"),
                                         start=True, stop=True).then_inc(spread, 1)
                    if c in (3, 4) and a3.ends():
                        g = a3.group()
                        pe.wait_ge(rt_ready, g * 2 + 2)
                        pe.wait_ge(counts_ready, g + 1)
                        pe.wait_ge(wl_ready, 2)
                        wait(pe, u_ready, upto(w, R))
                        for r in HALVES[c - 3]:
                            tile = slice(r * P, (r + 1) * P)
                            for n, (a, b) in enumerate(((0, wl_hi), (0, wl_lo), (1, wl_hi))):
                                for k in range(K):
                                    nc.tensor.matmul(ps_a[r // 2][:, r % 2, :], rt[:, a, k, tile], b[:, k, :],
                                                     start=(n == 0 and k == 0), stop=False)
                            nc.tensor.matmul(ps_a[r // 2][:, r % 2, :], counts[:, tile], lab_hi[:, :], start=False, stop=False)
                            mm = nc.tensor.matmul(ps_a[r // 2][:, r % 2, :], counts[:, tile], lab_lo[:, :], start=False, stop=True)
                            if r % 2:
                                mm.then_inc(mapped, 1)
                    if c == 6 and w.there():
                        pe.wait_ge(h_lo_ready, w.done(1, 1))
                        wait(pe, scored, upto(s, R))
                        wait(pe, pt_ready, upto(w, 1))
                        if a3.ends():
                            pe.wait_ge(rt_ready, a3.group() * 2 + 2)
                        turn(ps_s, h_hi, ps_t_k, h_lo, h_turned)
                    if c == 7 and a2.ends():
                        g = a2.group()
                        if a3.ends():
                            pe.wait_ge(result_ready, g * 2 - 1)
                        pe.wait_ge(onehot_ready, g * 2 + 2)
                        wait(pe, u_ready, upto(w, R))
                        for l in range(LABELS // 2):
                            mm = nc.tensor.matmul(ps_counts, pick[:, l, :], onehot[:, l, :],
                                                  start=(l == 0), stop=(l == LABELS // 2 - 1))
                        mm.then_inc(counted, 1)
                    if c < FFN_LAG and v.there():
                        second_product(v, c + C - FFN_LAG)
                    if c >= FFN_LAG and now.there():
                        second_product(now, c - FFN_LAG)

            program(pe, body)


def kernel(x, adj, L0_gnn_attn_w, L0_gnn_attn_b, L0_gnn_W1, L0_gnn_b1, L0_gnn_W2, L0_gnn_b2, L0_gnn_g1, L0_gnn_beta1,
           L0_gnn_g2, L0_gnn_beta2, L1_gnn_weights, L1_gnn_bias):
    import concourse.bacc as bacc
    import numpy as np
    from concourse.bass_utils import run_bass_kernel_spmd

    x, adj = np.asarray(x), np.asarray(adj)
    graphs = P // N * R

    def by_partition(a):
        a = np.asarray(a)
        return a.reshape(a.shape[0], -1, P).transpose(2, 0, 1)

    def row(a):
        return np.asarray(a).reshape(1, -1)

    arrays = {
        "x": x.reshape(-1, D),
        "adj": adj.reshape(-1, N),
        "adj_t": adj.reshape(-1, graphs, N, N).transpose(0, 3, 1, 2).reshape(-1, N, ROWS),
        "attn_w": row(L0_gnn_attn_w),
        "attn_b": row(L0_gnn_attn_b),
        "w1": L0_gnn_W1,
        "b1": by_partition(L0_gnn_b1),
        "w2": L0_gnn_W2,
        "b2": row(L0_gnn_b2),
        "g1": by_partition(L0_gnn_g1),
        "g1_row": row(L0_gnn_g1),
        "beta1": by_partition(L0_gnn_beta1),
        "beta1_row": row(L0_gnn_beta1),
        "g2": row(L0_gnn_g2),
        "beta2": row(L0_gnn_beta2),
        "wl": np.asarray(L1_gnn_weights).transpose(2, 0, 1).reshape(K, P, -1, D).transpose(1, 0, 2, 3).reshape(P, -1, D),
        "lab": L1_gnn_bias,
    }
    arrays = {f"in_{n}": np.ascontiguousarray(a) for n, a in arrays.items()}
    nc = bacc.Bacc("TRN2", target_bir_lowering=False, num_devices=1)
    args = [nc.dram_tensor(n, a.shape, mybir.dt.from_np(a.dtype), kind="ExternalInput").ap() for n, a in arrays.items()]
    out = nc.dram_tensor("out", arrays["in_x"].shape, F32, kind="ExternalOutput").ap()
    gnn_block(nc, *args, out)
    got = run_bass_kernel_spmd(nc, [arrays], core_ids=[0]).results[0]["out"]
    return got.reshape(x.shape)
```

```python
from contextlib import ExitStack

import concourse.bass as bass
from concourse import mybir

F32 = mybir.dt.float32
F16 = mybir.dt.float16
I32 = mybir.dt.int32
ALU = mybir.AluOpType
ACT = mybir.ActivationFunctionType
AX_X = mybir.AxisListType.X

P = 128
N = 64
D = 256
K = D // P
F = 4 * D
C = F // P
L = 3
LABELS = 16
LO = 32
R = 4
ROWS = R * P
EPS = 1e-5
SLOPE = 0.2
RING = 4
TEAM = 4
TURN = L * TEAM
MASKED = -1e30
SA = 16.0
SP = 256.0
SW = 64.0
SL = 16.0
FFN_LAG = 3


class Unit:

    def __init__(self, B, j, units):
        self.B, self.j, self.units = B, j, units
        self.fixed = isinstance(B, int)
        self.p = j // TEAM % L

    def there(self):
        return not self.fixed or 0 <= self.B * TURN + self.j < self.units

    def group(self):
        return self.B * TEAM + (self.j // TURN * TEAM + self.j % TEAM)

    def turns_of_two(self):
        return self.B * (TEAM // 2) + ((self.j // TURN * TEAM + self.j % TEAM) // 2 + 1)

    def ends(self):
        return self.p == L - 1 and self.there()

    def starts(self):
        return self.p == 0 and self.there()

    def done(self, each, n=0):
        if not self.fixed:
            return self.B * (TURN * each) + (self.j * each + n)
        k = self.B * TURN + self.j
        return min(max(k, 0), self.units) * each + (n if self.there() else 0)


def gnn_block(nc, x, adj, adjt_g, attn_w, attn_b, w1, b1, w2, b2, g1, g1_row, beta1, beta1_row, g2, beta2, wl, lab, out):
    G = x.shape[0] // ROWS

    x_g = x.rearrange("(g r p) d -> g p r d", r=R, p=P)
    adj_g = adj.rearrange("(g r p) n -> g p r n", r=R, p=P)
    out_g = out.rearrange("(g r p) d -> g p r d", r=R, p=P)

    ctx = ExitStack()
    with ctx:
        def sb(name, shape, dt=F32):
            return ctx.enter_context(nc.sbuf_tensor(name, shape, dt))

        def psum(name, shape, dt=F32):
            return ctx.enter_context(nc.psum_tensor(name, shape, dt))

        def sem(name):
            return ctx.enter_context(nc.semaphore(name))

        w1_hi = sb("w1_hi", [P, L, K, F], F16)
        w1_lo = sb("w1_lo", [P, L, K, F], F16)
        w2_hi = sb("w2_hi", [P, L, C, D], F16)
        w2_lo = sb("w2_lo", [P, L, C, D], F16)
        wl_hi = sb("wl_hi", [P, K, D], F16)
        wl_lo = sb("wl_lo", [P, K, D], F16)
        lab_halves = sb("lab_halves", [LO + LABELS, D], F16)
        lab_hi = sb("lab_hi", [LO + LABELS, D], F16)
        stage1 = [sb(f"stage1_{i}", [P, K, F]) for i in range(2)]
        stage2 = sb("stage2", [P, C, D])
        lab_f = sb("lab_f", [LO + LABELS, D])
        g1_r = sb("g1_r", [P, L, D])
        c1_r = sb("c1_r", [P, L, D])
        b2_r = sb("b2_r", [P, L, D])
        g2_r = sb("g2_r", [P, L, D])
        beta2_r = sb("beta2_r", [P, L, D])
        attn_r = sb("attn_r", [P, L, 2, D])
        attn_b_r = sb("attn_b_r", [P, L])
        g1_c = sb("g1_c", [P, L, K])
        g1_s = sb("g1_s", [P, L, K])
        beta1_c = sb("beta1_c", [P, L, K])
        b1_c = sb("b1_c", [P, L, C])
        b1_f = sb("b1_f", [P, L, C])
        ident = sb("ident", [P, P], F16)
        blocks = sb("blocks", [P, P])
        delta = sb("delta", [P, N])
        wl_eye = sb("wl_eye", [P, K, D])
        labels = sb("labels", [P, LABELS // 2])
        pick = sb("pick", [P, LABELS // 2, LO + LABELS], F16)
        half = sb("half", [P, R])
        x_in = [sb(f"x_in{i}", [P, R, D]) for i in range(2)]
        adj_in = sb("adj_in", [P, R, N], I32)
        adjt_in = sb("adjt_in", [P, ROWS], I32)
        adj_f = sb("adj_f", [P, R, N])
        off = [sb(f"off{i}", [P, R, N]) for i in range(TEAM)]
        xs = [sb(f"xs{i}", [P, R, D]) for i in range(3)]
        x_hi = sb("x_hi", [P, R, D], F16)
        x_lo = sb("x_lo", [P, R, D], F16)
        s_ij = sb("s_ij", [P, 2, 2, R])
        dots_junk = sb("dots_junk", [P, 2, D])
        diag = sb("diag", [P, R, N])
        score = sb("score", [P, R, N])
        leaky = sb("leaky", [P, R, N])
        row_max = sb("row_max", [P, R])
        shifted = sb("shifted", [P, R, N])
        expd = sb("expd", [P, R, N])
        row_sum = sb("row_sum", [P, R])
        row_sum_s = sb("row_sum_s", [P, R])
        inv_sum = sb("inv_sum", [P, 2, R])
        p_hi = sb("p_hi", [P, R, P], F16)
        p_lo = sb("p_lo", [P, R, P], F16)
        pt = sb("pt", [P, 2, R, P], F16)
        u = sb("u", [P, R, D])
        h = u
        h_hi = sb("h_hi", [P, R, D], F16)
        h_lo = sb("h_lo", [P, R, D], F16)
        ht = [sb(f"ht{i}", [P, 2, K, ROWS], F16) for i in range(2)]
        hb = [sb(f"hb{i}", [P, R, D]) for i in range(2)]
        act32 = sb("act32", [P, RING, ROWS])
        act_hi = sb("act_hi", [P, RING, ROWS], F16)
        act_lo = sb("act_lo", [P, RING, ROWS], F16)
        y = sb("y", [P, R, D])
        xn = y
        LNS = 5
        LN_Y, LN_U, LN_LAST, *LN_IN = range(LNS)
        stats = sb("stats", [P, LNS, R, 6])
        mv = sb("mv", [P, LNS, R, 2])
        var = sb("var", [P, LNS, R])
        neg_mean = sb("neg_mean", [P, LNS, R])
        rstd = sb("rstd", [P, LNS, R])
        shift = sb("shift", [P, LNS, R])
        x2 = [sb(f"x2_{i}", [P, R, D]) for i in range(2)]
        r_hi = sb("r_hi", [P, R, D], F16)
        r_lo = sb("r_lo", [P, R, D], F16)
        rt = sb("rt", [P, 2, K, ROWS], F16)
        adjt_h = sb("adjt_h", [P, ROWS], F16)
        x_again = stage1[1][:, 0, :].rearrange("p (r d) -> p r d", r=R)
        onehot = stage2[:, :, :].bitcast(F16).rearrange("p l (s d) -> p (l s d)", s=2).rearrange("p (l r) -> p l r", r=ROWS)
        counts = sb("counts", [LO + LABELS, ROWS], F16)
        last_n = stage1[0][:, 0, :].rearrange("p (r d) -> p r d", r=R)
        result = stage1[0][:, 1, :].rearrange("p (r d) -> p r d", r=R)

        ps_h = [psum(f"ps_h{i}", [P, ROWS]) for i in range(2)]
        ps_f = [psum(f"ps_f{i}", [P, 2, D]) for i in range(2)]
        ps_a = [psum(f"ps_a{i}", [P, 2, D]) for i in range(2)]
        ps_s = psum("ps_s", [P, K, ROWS], F16)
        ps_t = psum("ps_t", [P, 2 * ROWS], F16)
        ps_s32 = ps_s[:, :, :].rearrange("p k r -> p (k r)").bitcast(F32)
        ps_b1 = (ps_f[0][:, 0, :], ps_f[1][:, 0, :], ps_h[1][:, :])
        ps_counts = (ps_h[1][0:LO + LABELS, :], ps_a[0][0:LO + LABELS, :, :].rearrange("p s d -> p (s d)"))

        columns_in = sem("columns_in")
        attn_in = sem("attn_in")
        rows_in = sem("rows_in")
        stage1_in = [sem(f"stage1_in{i}") for i in range(2)]
        stage2_in = sem("stage2_in")
        lab_in = sem("lab_in")
        x_loaded = [sem(f"x_loaded{i}") for i in range(2)]
        adj_loaded = sem("adj_loaded")
        x_again_loaded = sem("x_again_loaded")
        adjt_loaded = sem("adjt_loaded")
        stored = [sem(f"stored{i}") for i in range(2)]
        masks = sem("masks")
        halves_set = sem("halves_set")
        c1_ready = sem("c1_ready")
        rows_scaled = sem("rows_scaled")
        g1s_ready = sem("g1s_ready")
        w1_hi_ready = sem("w1_hi_ready")
        w1_lo_ready = sem("w1_lo_ready")
        w2_hi_ready = sem("w2_hi_ready")
        w2_lo_ready = sem("w2_lo_ready")
        b1_summed = sem("b1_summed")
        b1_ready = sem("b1_ready")
        wl_steps = sem("wl_steps")
        wl_hi_ready = sem("wl_hi_ready")
        wl_ready = sem("wl_ready")
        in_stats = sem("in_stats")
        in_mv = sem("in_mv")
        in_var = sem("in_var")
        in_rstd = sem("in_rstd")
        in_ready = sem("in_ready")
        adj_f_ready = sem("adj_f_ready")
        off_ready = sem("off_ready")
        dots_ready = sem("dots_ready")
        diag_ready = sem("diag_ready")
        spread = sem("spread")
        scored = sem("scored")
        leaked = sem("leaked")
        max_ready = sem("max_ready")
        shift_ready = sem("shift_ready")
        exp_ready = sem("exp_ready")
        sum_ready = sem("sum_ready")
        sum_scaled = sem("sum_scaled")
        inv_ready = sem("inv_ready")
        p_hi_ready = sem("p_hi_ready")
        p_lo_ready = sem("p_lo_ready")
        p_turned = sem("p_turned")
        pt_ready = sem("pt_ready")
        x_hi_ready = sem("x_hi_ready")
        x_lo_ready = sem("x_lo_ready")
        mixed = sem("mixed")
        u_ready = sem("u_ready")
        u_stats = sem("u_stats")
        u_mv = sem("u_mv")
        u_var = sem("u_var")
        u_rstd = sem("u_rstd")
        h_ready = sem("h_ready")
        h_hi_ready = sem("h_hi_ready")
        h_lo_ready = sem("h_lo_ready")
        h_turned = sem("h_turned")
        ht_hi_ready = sem("ht_hi_ready")
        ht_lo_ready = sem("ht_lo_ready")
        hg_ready = sem("hg_ready")
        hb_ready = sem("hb_ready")
        hidden = sem("hidden")
        act_ready = sem("act_ready")
        act_hi_ready = sem("act_hi_ready")
        act_lo_ready = sem("act_lo_ready")
        second = sem("second")
        y_ready = sem("y_ready")
        y_stats = sem("y_stats")
        y_mv = sem("y_mv")
        y_var = sem("y_var")
        y_rstd = sem("y_rstd")
        xn_ready = sem("xn_ready")
        xg_ready = sem("xg_ready")
        x_ready = sem("x_ready")
        x_again_ready = sem("x_again_ready")
        last_stats = sem("last_stats")
        last_mv = sem("last_mv")
        last_var = sem("last_var")
        last_rstd = sem("last_rstd")
        last_norm = sem("last_norm")
        r_hi_ready = sem("r_hi_ready")
        r_lo_ready = sem("r_lo_ready")
        r_turned = sem("r_turned")
        rt_ready = sem("rt_ready")
        adjt_h_ready = sem("adjt_h_ready")
        onehot_ready = sem("onehot_ready")
        counted = sem("counted")
        counts_ready = sem("counts_ready")
        mapped = sem("mapped")
        result_ready = sem("result_ready")

        MASK_STEPS = 6
        HALVES = (range(0, R // 2), range(R // 2, R))
        U = G * L
        BEFORE, AFTER = 3, 3
        MEASURED_IN = {-3: 1, -2: 2, -1: 3, 5: 12, 7: 13, 10: 14, 11: 15}
        W1_SLOTS, W2_SLOTS, LAST_MAP_SLOT = {0: 1, 4: 2}, {2: 1, 6: 2}, 8

        def program(eng, body):
            for j in range(-BEFORE, TURN):
                body(0, j)
            with eng.Fori(1, G // TEAM - 1) as B:
                for j in range(TURN):
                    body(B, j)
            for j in range(TURN + AFTER):
                body(G // TEAM - 1, j)

        def part(k):
            return slice(k * (C // K), (k + 1) * (C // K))

        def upto(v, each):
            return v.done(each, each)

        block = ctx.enter_context(nc.Block())

        def wait(eng, semaphore, value):
            if not isinstance(value, int) or value > 0:
                eng.wait_ge(semaphore, value)

        @block.sync
        def _(sp):
            def load_columns():
                for tile, row in ((g1_c, g1), (beta1_c, beta1), (b1_c, b1)):
                    sp.dma_start(tile[:, :, :], row).then_inc(columns_in, 16)

            def load_attention():
                sp.dma_start(attn_r[:, :, :, :].rearrange("p l s d -> p (l s d)"), attn_w.to_broadcast([P, L * 2 * D])).then_inc(attn_in, 16)
                sp.dma_start(attn_b_r[:, :], attn_b.to_broadcast([P, L])).then_inc(attn_in, 16)

            def load_rows():
                for tile, row in ((g1_r, g1_row), (c1_r, beta1_row), (b2_r, b2), (g2_r, g2), (beta2_r, beta2)):
                    sp.dma_start(tile[:, :, :].rearrange("p l d -> p (l d)"), row.to_broadcast([P, L * D])).then_inc(rows_in, 16)

            def load_w1(l):
                if l >= 2:
                    sp.wait_ge(w1_lo_ready, K * (l - 1))
                    sp.wait_ge(b1_summed, l - 1)
                sp.dma_start(stage1[l % 2][:, :, :], w1[l].rearrange("(k p) f -> p k f", p=P)).then_inc(stage1_in[l % 2], 16)

            def load_w2(l):
                wait(sp, w2_lo_ready, K * l)
                sp.dma_start(stage2[:, :, :], w2[l].rearrange("(c p) d -> p c d", p=P)).then_inc(stage2_in, 16)

            def load_last_map():
                sp.wait_ge(w2_lo_ready, K * L)
                sp.dma_start(stage2[:, 0:2 * K, :], wl).then_inc(stage2_in, 16)
                for first in (0, LO):
                    sp.dma_start(lab_f[first:first + LABELS, :], lab).then_inc(lab_in, 16)

            def body(B, j):
                e, v, a3 = (Unit(B, j + i, U) for i in (3, -1, -3))
                coming = Unit(B, MEASURED_IN.get(j, -1), U)
                if j == -BEFORE:
                    sp.dma_start(x_in[e.j % 2][:, :, :], x_g[0]).then_inc(x_loaded[e.j % 2], 16)
                if j in MEASURED_IN and coming.there():
                    n = coming.group()
                    wait(sp, in_ready, (n - 1) * R)
                    sp.dma_start(x_in[coming.j % 2][:, :, :], x_g[n]).then_inc(x_loaded[coming.j % 2], 16)
                if e.starts():
                    n = e.group()
                    wait(sp, adj_f_ready, n)
                    sp.dma_start(adj_in[:, :, :], adj_g[n]).then_inc(adj_loaded, 16)
                if j == -BEFORE:
                    load_columns()
                    load_attention()
                    load_w1(0)
                    load_w2(0)
                    load_w1(1)
                    load_rows()
                if j == -2:
                    load_w1(2)
                if e.fixed and B == 0 and j in W2_SLOTS:
                    load_w2(W2_SLOTS[j])
                if e.fixed and B == 0 and j == LAST_MAP_SLOT:
                    load_last_map()
                if v.ends():
                    n = v.group()
                    wait(sp, x_ready, Unit(B, j - 2, U).done(2, 2))
                    sp.dma_start(x_again[:, :, :], x_g[n]).then_inc(x_again_loaded, 16)
                    wait(sp, adjt_h_ready, n)
                    for s in range(2):
                        sp.dma_start(adjt_in[s * N:(s + 1) * N, :], adjt_g[n]).then_inc(adjt_loaded, 16)
                if a3.ends():
                    g = a3.group()
                    for i in range(2):
                        sp.wait_ge(result_ready, g * 2 + i + 1)
                        sp.dma_start(out_g[g][:, 2 * i:2 * i + 2, :], result[:, 2 * i:2 * i + 2, :]).then_inc(stored[i], 16)

            program(sp, body)
            for i in range(2):
                sp.wait_ge(stored[i], 16 * G)

        @block.gpsimd
        def _(pool):
            def mark(view, pattern, base):
                return nc.gpsimd.affine_select(out=view, in_=view, compare_op=ALU.not_equal, fill=1.0, base=base,
                                               pattern=pattern, channel_multiplier=1)

            nc.gpsimd.memset(half[:, :], -0.5)
            nc.gpsimd.memset(delta[:, :], 0.0)
            nc.gpsimd.memset(ident[:, :], 0.0)
            nc.gpsimd.memset(wl_eye[:, :, :], 0.0)
            nc.gpsimd.memset(blocks[:, :], 0.0)
            nc.gpsimd.memset(pick[:, :, :], 0.0)
            nc.gpsimd.memset(lab_halves[:, :], 0.0)
            nc.gpsimd.memset(p_hi[:, :, :], 0.0)
            nc.gpsimd.memset(p_lo[:, :, :], 0.0).then_inc(masks, 1)
            pool.wait_ge(masks, 1)
            mark(delta[:, :], [[-1, N]], 0).then_inc(masks, 1)
            pool.wait_ge(masks, 2)
            mark(delta[:, :], [[-1, N]], -N).then_inc(masks, 1)
            mark(ident[:, :], [[-1, P]], 0).then_inc(masks, 1)
            mark(wl_eye[:, 0, :], [[-1, D]], 0).then_inc(masks, 1)
            mark(wl_eye[:, 1, :], [[-1, D]], P).then_inc(masks, 1)
            pool.wait_ge(masks, MASK_STEPS)

            def rows_of(tile, l, tiles=R):
                return tile[:, l, :].unsqueeze(1).to_broadcast([P, tiles, D])

            def scale_and_shift(ln, done, value):
                nc.gpsimd.tensor_tensor(rstd[:, ln, :], var[:, ln, :], half[:, :], ALU.pow).then_inc(done, 1)
                pool.wait_ge(done, value)
                nc.gpsimd.tensor_tensor(shift[:, ln, :], neg_mean[:, ln, :], rstd[:, ln, :], ALU.mult).then_inc(done, 1)

            def body(B, j):
                a2, v, now, w, s, e = (Unit(B, j + i, U) for i in (-2, -1, 0, 1, 2, 3))
                if e.starts():
                    n = e.group()
                    pool.wait_ge(in_var, n * 2 + 2)
                    wait(pool, in_ready, (n - 1) * R)
                    scale_and_shift(LN_IN[e.j % 2], in_rstd, n * 2 + 1)
                if j == -1:
                    pool.wait_ge(rows_in, 16 * 5)
                    nc.gpsimd.tensor_tensor(c1_r[:, :, :], c1_r[:, :, :], b2_r[:, :, :], ALU.add).then_inc(c1_ready, 1)
                    pool.wait_ge(c1_ready, 1)
                if s.there():
                    pool.wait_ge(dots_ready, s.done(2 * R, 2 * R))
                    wait(pool, spread, s.done(1))
                    nc.gpsimd.tensor_tensor(diag[:, :, :], delta[:, :].unsqueeze(1).to_broadcast([P, R, N]),
                                            s_ij[:, s.j % 2, 1, :].unsqueeze(2).to_broadcast([P, R, N]), ALU.mult).then_inc(diag_ready, 1)
                if v.ends():
                    g = v.group()
                    pool.wait_ge(x_again_loaded, g * 16 + 16)
                    nc.gpsimd.tensor_tensor(x_again[:, :, :], x_again[:, :, :], rows_of(beta2_r, L - 1), ALU.add).then_inc(x_again_ready, 1)
                if a2.ends():
                    g = a2.group()
                    pool.wait_ge(last_var, g * 2 + 2)
                    scale_and_shift(LN_LAST, last_rstd, g * 2 + 1)
                if w.there():
                    pool.wait_ge(u_var, w.done(2, 2))
                    scale_and_shift(LN_U, u_rstd, w.done(2, 1))
                if s.there():
                    pool.wait_ge(x_hi_ready, s.done(1, 1))
                    wait(pool, mixed, s.done(2))
                    nc.gpsimd.tensor_tensor(x_lo[:, :, :], xs[s.j % 3][:, :, :], x_hi[:, :, :], ALU.subtract).then_inc(x_lo_ready, 1)
                if w.there():
                    pool.wait_ge(h_ready, w.done(R, R))
                    wait(pool, y_ready, upto(v, 2))
                    nc.gpsimd.tensor_tensor(hb[w.j % 2][:, :, :], h[:, :, :], rows_of(g1_r, w.p), ALU.mult).then_inc(hg_ready, 1)
                if v.there():
                    pool.wait_ge(y_var, v.done(2, 2))
                    scale_and_shift(LN_Y, y_rstd, v.done(2, 1))
                if w.there():
                    pool.wait_ge(hg_ready, w.done(1, 1))
                    nc.gpsimd.tensor_tensor(hb[w.j % 2][:, :, :], hb[w.j % 2][:, :, :], rows_of(c1_r, w.p), ALU.add).then_inc(hb_ready, 1)
                if a2.ends() and now.there():
                    g = a2.group()
                    pool.wait_ge(r_hi_ready, g + 1)
                    wait(pool, r_turned, g * 2)
                    nc.gpsimd.tensor_tensor(r_lo[:, :, :], last_n[:, :, :], r_hi[:, :, :], ALU.subtract).then_inc(r_lo_ready, 1)
                if now.fixed and B == 0 and j == 1:
                    pool.wait_ge(rows_scaled, 2)
                if v.there():
                    if v.p < L - 1:
                        to, rest = xs[j % 3], rows_of(beta2_r, v.p)
                        wait(pool, u_ready, upto(now, R))
                    else:
                        to, rest = x2[v.j % 2], x_again[:, :, :]
                        wait(pool, result_ready, (v.group() - 1) * 2)
                    for i in range(2):
                        half_rows = slice(2 * i, 2 * i + 2)
                        pool.wait_ge(xn_ready, v.done(R, R // 2 * (i + 1)))
                        nc.gpsimd.tensor_tensor(to[:, half_rows, :], xn[:, half_rows, :], rows_of(g2_r, v.p, 2), ALU.mult).then_inc(xg_ready, 1)
                        pool.wait_ge(xg_ready, v.done(2, i + 1))
                        if v.p == L - 1 and i == 0:
                            pool.wait_ge(x_again_ready, v.group() + 1)
                        nc.gpsimd.tensor_tensor(to[:, half_rows, :], to[:, half_rows, :], rest[:, half_rows, :], ALU.add).then_inc(x_ready, 1)

            program(pool, body)

        @block.scalar
        def _(act):
            def prepare_w1(l, chunks):
                act.wait_ge(g1s_ready, 1)
                act.wait_ge(stage1_in[l % 2], 16 * (l // 2 + 1))
                for k in chunks:
                    nc.scalar.activation(w1_hi[:, l, k, :], stage1[l % 2][:, k, :], ACT.Copy,
                                         scale=g1_s[:, l, k:k + 1]).then_inc(w1_hi_ready, 1)

            def prepare_w2(l, chunks):
                act.wait_ge(stage2_in, 16 * (l + 1))
                for k in chunks:
                    nc.scalar.activation(w2_hi[:, l, part(k), :], stage2[:, part(k), :], ACT.Copy, scale=SW).then_inc(w2_hi_ready, 1)

            def prepare_last():
                act.wait_ge(wl_steps, 2)
                nc.scalar.activation(wl_hi[:, :, :], wl_eye[:, :, :], ACT.Copy, scale=SL).then_inc(wl_hi_ready, 1)
                act.wait_ge(lab_in, 16 * 2)
                for first, to in ((0, lab_halves), (LO, lab_hi)):
                    rows = slice(first, first + LABELS)
                    nc.scalar.activation(to[rows, :], lab_f[rows, :], ACT.Copy, scale=SL).then_inc(wl_hi_ready, 1)

            def body(B, j):
                a3, a2, v, now, w, s, e = (Unit(B, j + i, U) for i in (-3, -2, -1, 0, 1, 2, 3))
                for c in range(C):
                    if c == 3 and w.there():
                        act.wait_ge(u_rstd, w.done(2, 2))
                        for r in HALVES[0]:
                            nc.scalar.activation(h[:, r, :], u[:, r, :], ACT.Identity, bias=shift[:, LN_U, r:r + 1],
                                                 scale=rstd[:, LN_U, r:r + 1]).then_inc(h_ready, 1)
                    if c == 6 and w.there():
                        act.wait_ge(h_turned, w.done(2, 1))
                        nc.scalar.activation(ht[w.j % 2][:, 0, :, :], ps_s[:, :, :], ACT.Copy).then_inc(ht_hi_ready, 1)
                    if now.there():
                        if now.fixed and c == 0:
                            act.wait_ge(b1_ready, now.p + 1)
                        act.wait_ge(hidden, now.done(C, c + 1))
                        wait(act, act_lo_ready, now.done(C, c + 1 - RING))
                        nc.scalar.activation(act32[:, c % RING, :], ps_h[c % 2][:, :], ACT.Gelu, bias=b1_f[:, now.p, c:c + 1],
                                             scale=1.0 / (SA * SW)).then_inc(act_ready, 1)
                        act.wait_ge(act_ready, now.done(C, c + 1))
                        wait(act, second, now.done(2 * C, 2 * (c + 1 - RING)))
                        nc.scalar.activation(act_hi[:, c % RING, :], act32[:, c % RING, :], ACT.Copy, scale=SA).then_inc(act_hi_ready, 1)
                    if c == 0 and a3.ends():
                        g = a3.group()
                        act.wait_ge(counted, g + 1)
                        nc.scalar.activation(counts[:, :], ps_counts[v.there()], ACT.Copy, scale=SL).then_inc(counts_ready, 1)
                    if c == 0 and w.there():
                        act.wait_ge(p_turned, w.done(1, 1))
                        wait(act, mixed, w.done(2))
                        nc.scalar.activation(pt[:, :, :, :].rearrange("p s r i -> p (s r i)"), ps_t[:, :],
                                             ACT.Copy).then_inc(pt_ready, 1)
                    if c == 1 and a3.ends():
                        g = a3.group()
                        act.wait_ge(r_turned, g * 2 + 1)
                        nc.scalar.activation(rt[:, 0, :, :], ps_s[:, :, :], ACT.Copy).then_inc(rt_ready, 1)
                        act.wait_ge(r_turned, g * 2 + 2)
                        nc.scalar.activation(rt[:, 1, :, :].rearrange("p k r -> p (k r)"), ps_t[:, :],
                                             ACT.Copy).then_inc(rt_ready, 1)
                    if c == 1 and s.there():
                        if s.p == 0:
                            act.wait_ge(in_ready, s.group() * R + R)
                        else:
                            act.wait_ge(x_ready, a2.done(2, 2))
                        wait(act, mixed, s.done(2))
                        nc.scalar.activation(x_hi[:, :, :], xs[s.j % 3][:, :, :], ACT.Copy).then_inc(x_hi_ready, 1)
                    if c == 3 and w.there():
                        for r in HALVES[1]:
                            nc.scalar.activation(h[:, r, :], u[:, r, :], ACT.Identity, bias=shift[:, LN_U, r:r + 1],
                                                 scale=rstd[:, LN_U, r:r + 1]).then_inc(h_ready, 1)
                    if c == 4 and s.there():
                        act.wait_ge(shift_ready, s.done(1, 1))
                        wait(act, p_lo_ready, s.done(2))
                        nc.scalar.activation(expd[:, :, :], shifted[:, :, :], ACT.Exp).then_inc(exp_ready, 1)
                    if c == 5 and v.there():
                        act.wait_ge(y_rstd, v.done(2, 2))
                        for r in range(R):
                            nc.scalar.activation(xn[:, r, :], y[:, r, :], ACT.Identity, bias=shift[:, LN_Y, r:r + 1],
                                                 scale=rstd[:, LN_Y, r:r + 1]).then_inc(xn_ready, 1)
                    if c == 6 and w.there() and (a2.ends() or a3.ends()):
                        act.wait_ge(h_turned, w.done(2, 2))
                        nc.scalar.activation(ht[w.j % 2][:, 1, :, :].rearrange("p k r -> p (k r)"), ps_t[:, :],
                                             ACT.Copy).then_inc(ht_lo_ready, 1)
                    if c in (1, 2) and e.starts():
                        n = e.group()
                        act.wait_ge(in_rstd, n * 2 + 2)
                        wait(act, u_ready, upto(now, R))
                        for r in HALVES[c - 1]:
                            nc.scalar.activation(xs[j % 3][:, r, :], x_in[e.j % 2][:, r, :], ACT.Relu, bias=shift[:, LN_IN[e.j % 2], r:r + 1],
                                                 scale=rstd[:, LN_IN[e.j % 2], r:r + 1]).then_inc(in_ready, 1)
                    if c == (2 if now.there() else 6) and a2.ends():
                        g = a2.group()
                        act.wait_ge(last_rstd, g * 2 + 2)
                        wait(act, r_lo_ready, g)
                        for r in range(R):
                            nc.scalar.activation(last_n[:, r, :], x2[a2.j % 2][:, r, :], ACT.Relu, bias=shift[:, LN_LAST, r:r + 1],
                                                 scale=rstd[:, LN_LAST, r:r + 1]).then_inc(last_norm, 1)
                        act.wait_ge(last_norm, g * R + R)
                        wait(act, r_turned, g * 2)
                        nc.scalar.activation(r_hi[:, :, :], last_n[:, :, :], ACT.Copy).then_inc(r_hi_ready, 1)
                    if c == 3 and j == -BEFORE:
                        prepare_w1(0, range(K))
                        prepare_w2(0, range(K))
                    if c == 2 and now.fixed and B == 0:
                        for k in range(K):
                            if j - k in W1_SLOTS:
                                prepare_w1(W1_SLOTS[j - k], (k,))
                            if j - k in W2_SLOTS:
                                prepare_w2(W2_SLOTS[j - k], (k,))
                    if c == 7 and now.fixed and B == 0 and j == LAST_MAP_SLOT:
                        prepare_last()

            program(act, body)

        @block.vector
        def _(dve):
            dve.wait_ge(masks, 1)
            for s in range(2):
                rows = slice(s * N, (s + 1) * N)
                nc.vector.memset(blocks[rows, rows], 1.0)
                for l in range(LABELS // 2):
                    label = l + s * (LABELS // 2)
                    nc.vector.memset(labels[rows, l:l + 1], float(label))
                    for first in (0, LO):
                        set_last = nc.vector.memset(pick[rows, l, first + label:first + label + 1], 1.0)
            set_last.then_inc(halves_set, 1)
            dve.wait_ge(masks, MASK_STEPS)
            dve.wait_ge(halves_set, 1)

            def prepare_w1(l, chunks):
                for k in chunks:
                    dve.wait_ge(w1_hi_ready, K * l + k + 1)
                    nc.vector.scalar_tensor_tensor(out=w1_lo[:, l, k, :], in0=stage1[l % 2][:, k, :], scalar=g1_s[:, l, k:k + 1],
                                                   in1=w1_hi[:, l, k, :], op0=ALU.mult, op1=ALU.subtract).then_inc(w1_lo_ready, 1)

            def prepare_w2(l, chunks):
                for k in chunks:
                    dve.wait_ge(w2_hi_ready, K * l + k + 1)
                    nc.vector.scalar_tensor_tensor(out=w2_lo[:, l, part(k), :], in0=stage2[:, part(k), :], scalar=SW, in1=w2_hi[:, l, part(k), :],
                                                   op0=ALU.mult, op1=ALU.subtract).then_inc(w2_lo_ready, 1)

            def prepare_b1(l):
                dve.wait_ge(b1_summed, l + 1)
                nc.vector.tensor_tensor(b1_f[:, l, :], ps_b1[l][:, 0:C], b1_c[:, l, :], ALU.add).then_inc(b1_ready, 1)

            def prepare_last():
                dve.wait_ge(stage2_in, 16 * (L + 1))
                both = stage2[:, 0:2 * K, :].rearrange("p (k s) o -> p k s o", s=2)
                for s in range(2):
                    wait(dve, wl_steps, s)
                    nc.vector.tensor_tensor(wl_eye[:, :, :], wl_eye[:, :, :], both[:, :, s, :], ALU.add).then_inc(wl_steps, 1)
                dve.wait_ge(wl_hi_ready, 3)
                nc.vector.scalar_tensor_tensor(out=wl_lo[:, :, :], in0=wl_eye[:, :, :], scalar=SL, in1=wl_hi[:, :, :],
                                               op0=ALU.mult, op1=ALU.subtract).then_inc(wl_ready, 1)
                low = slice(LO, LO + LABELS)
                nc.vector.scalar_tensor_tensor(out=lab_halves[low, :], in0=lab_f[low, :], scalar=SL, in1=lab_hi[low, :],
                                               op0=ALU.mult, op1=ALU.subtract).then_inc(wl_ready, 1)

            def statistics(ln, of, done):
                for r in range(R):
                    nc.vector.bn_stats(stats[:, ln, r, :], of[:, r, :]).then_inc(done, 1)

            def aggregate(ln, mv_done, mv_value, var_done, eps=EPS, scale=1.0):
                for r in range(R):
                    nc.vector.bn_aggr(mv[:, ln, r, :], stats[:, ln, r, :]).then_inc(mv_done, 1)
                dve.wait_ge(mv_done, mv_value)
                nc.vector.tensor_scalar(var[:, ln, :], mv[:, ln, :, 1], eps, scale, ALU.add, ALU.mult).then_inc(var_done, 1)
                nc.vector.tensor_scalar(neg_mean[:, ln, :], mv[:, ln, :, 0], -1.0, None, ALU.mult).then_inc(var_done, 1)

            def body(B, j):
                a3, a2, v, now, w, s, e = (Unit(B, j + i, U) for i in (-3, -2, -1, 0, 1, 2, 3))
                for c in range(C):
                    if c == 0 and j == -2:
                        dve.wait_ge(attn_in, 16 * 2)
                    if c in (0, 1) and s.there():
                        if s.p == 0:
                            dve.wait_ge(in_ready, s.group() * R + R // 2 * (c + 1))
                        else:
                            dve.wait_ge(x_ready, a2.done(2, c + 1))
                        for r in HALVES[c]:
                            for i in range(2):
                                wait(dve, dots_ready, s.done(2 * R, 2 * r + i - 1))
                                nc.vector.tensor_tensor_reduce(dots_junk[:, i, :], xs[s.j % 3][:, r, :], attn_r[:, s.p, i, :], 1.0 / SA,
                                                               attn_b_r[:, s.p:s.p + 1] if i == 0 else 0.0, ALU.mult, ALU.add,
                                                               s_ij[:, s.j % 2, i, r:r + 1]).then_inc(dots_ready, 1)
                    last_step = c == 1 and a2.ends()
                    if last_step:
                        dve.wait_ge(x_ready, a2.done(2, 2))
                        statistics(LN_LAST, x2[a2.j % 2], last_stats)
                    mix_step = c == 2 and w.there()
                    if mix_step:
                        wait(dve, hg_ready, w.done(1))
                        dve.wait_ge(inv_ready, w.done(1, 1))
                        for r in range(R):
                            if r % 2 == 0:
                                dve.wait_ge(mixed, w.done(2, r // 2 + 1))
                            nc.vector.scalar_tensor_tensor(out=u[:, r, :], in0=ps_a[r // 2][:, r % 2, :],
                                                           scalar=inv_sum[:, w.j % 2, r:r + 1], in1=xs[w.j % 3][:, r, :],
                                                           op0=ALU.mult, op1=ALU.add).then_inc(u_ready, 1)
                        dve.wait_ge(u_ready, w.done(R, R))
                        statistics(LN_U, u, u_stats)
                    tail_step = c == 3 and v.there()
                    if tail_step:
                        dve.wait_ge(hb_ready, v.done(1, 1))
                        wait(dve, xg_ready, v.done(2))
                        for i in range(2):
                            dve.wait_ge(second, v.done(2 * C, 2 * C - 1 + i))
                            nc.vector.scalar_tensor_tensor(out=y[:, 2 * i:2 * i + 2, :], in0=ps_f[i][:, :, :], scalar=1.0 / (SA * SW),
                                                           in1=hb[v.j % 2][:, 2 * i:2 * i + 2, :], op0=ALU.mult,
                                                           op1=ALU.add).then_inc(y_ready, 1)
                    if c == 3 and s.there():
                        dve.wait_ge(spread, s.done(1, 1))
                        dve.wait_ge(off_ready, s.group() + 1)
                        for r in range(R):
                            nc.vector.scalar_tensor_tensor(out=score[:, r, :], in0=ps_s32[:, r * N:(r + 1) * N],
                                                           scalar=s_ij[:, s.j % 2, 0, r:r + 1], in1=off[s.j % TEAM][:, r, :],
                                                           op0=ALU.add, op1=ALU.add).then_inc(scored, 1)
                        dve.wait_ge(scored, s.done(R, R))
                        nc.vector.scalar_tensor_tensor(out=leaky[:, :, :], in0=score[:, :, :], scalar=SLOPE, in1=score[:, :, :],
                                                       op0=ALU.mult, op1=ALU.max).then_inc(leaked, 1)
                        dve.wait_ge(leaked, s.done(1, 1))
                        nc.vector.tensor_reduce(row_max[:, :], leaky[:, :, :], AX_X, ALU.max).then_inc(max_ready, 1)
                        dve.wait_ge(max_ready, s.done(1, 1))
                        nc.vector.tensor_tensor(shifted[:, :, :], leaky[:, :, :], row_max[:, :].unsqueeze(2).to_broadcast([P, R, N]),
                                                ALU.subtract).then_inc(shift_ready, 1)
                    if tail_step:
                        dve.wait_ge(y_ready, v.done(2, 2))
                        statistics(LN_Y, y, y_stats)
                    if c == 4 and w.there():
                        dve.wait_ge(h_ready, w.done(R, R))
                        wait(dve, h_turned, w.done(2))
                        nc.vector.tensor_scalar(h_hi[:, :, :], h[:, :, :], SA, None, ALU.mult).then_inc(h_hi_ready, 1)
                        dve.wait_ge(h_hi_ready, w.done(1, 1))
                        nc.vector.scalar_tensor_tensor(out=h_lo[:, :, :], in0=h[:, :, :], scalar=SA, in1=h_hi[:, :, :],
                                                       op0=ALU.mult, op1=ALU.subtract).then_inc(h_lo_ready, 1)
                    if c in (5, 6) and a2.ends():
                        g = a2.group()
                        if c == 5:
                            dve.wait_ge(adjt_loaded, g * 32 + 32)
                            wait(dve, onehot_ready, g * 2)
                            nc.vector.tensor_copy(adjt_h[:, :], adjt_in[:, :]).then_inc(adjt_h_ready, 1)
                            dve.wait_ge(adjt_h_ready, g + 1)
                            wait(dve, counted, g)
                        for l in range(LABELS // 4) if c == 5 else range(LABELS // 4, LABELS // 2):
                            one = nc.vector.tensor_scalar(onehot[:, l, :], adjt_h[:, :], labels[:, l:l + 1], None, ALU.is_equal)
                        one.then_inc(onehot_ready, 1)
                    if c == 6 and s.there():
                        dve.wait_ge(exp_ready, s.done(1, 1))
                        wait(dve, p_turned, s.done(1))
                        nc.vector.tensor_reduce(row_sum[:, :], expd[:, :, :], AX_X, ALU.add).then_inc(sum_ready, 1)
                        for i in range(2):
                            rows = slice(i * N, (i + 1) * N)
                            nc.vector.tensor_scalar(p_hi[rows, :, rows], expd[rows, :, :], SP, None, ALU.mult).then_inc(p_hi_ready, 1)
                        for i in range(2):
                            rows = slice(i * N, (i + 1) * N)
                            dve.wait_ge(p_hi_ready, s.done(2, i + 1))
                            nc.vector.scalar_tensor_tensor(out=p_lo[rows, :, rows], in0=expd[rows, :, :], scalar=SP,
                                                           in1=p_hi[rows, :, rows], op0=ALU.mult,
                                                           op1=ALU.subtract).then_inc(p_lo_ready, 1)
                        dve.wait_ge(sum_ready, s.done(1, 1))
                        nc.vector.tensor_scalar(row_sum_s[:, :], row_sum[:, :], SP, None, ALU.mult).then_inc(sum_scaled, 1)
                        dve.wait_ge(sum_scaled, s.done(1, 1))
                        nc.vector.reciprocal(inv_sum[:, s.j % 2, :], row_sum_s[:, :]).then_inc(inv_ready, 1)
                    if c == 6 and w.there() and not (a2.ends() or a3.ends()):
                        dve.wait_ge(h_turned, w.done(2, 2))
                        nc.vector.tensor_copy(ht[w.j % 2][:, 1, :, :].rearrange("p k r -> p (k r)"), ps_t[:, :]).then_inc(ht_lo_ready, 1)
                    if c == 5 and e.starts():
                        n = e.group()
                        dve.wait_ge(adj_loaded, n * 16 + 16)
                        nc.vector.tensor_tensor(adj_f[:, :, :], adj_in[:, :, :], delta[:, :].unsqueeze(1).to_broadcast([P, R, N]),
                                                ALU.add).then_inc(adj_f_ready, 1)
                        dve.wait_ge(adj_f_ready, n + 1)
                        nc.vector.tensor_scalar(off[e.j % TEAM][:, :, :], adj_f[:, :, :], 0.0, MASKED, ALU.is_le, ALU.mult).then_inc(off_ready, 1)
                    if c in (5, 6) and a3.ends():
                        g = a3.group()
                        i = c - 5
                        wait(dve, stored[i], g * 16)
                        dve.wait_ge(mapped, g * 2 + i + 1)
                        nc.vector.scalar_tensor_tensor(out=result[:, 2 * i:2 * i + 2, :], in0=ps_a[i][:, :, :],
                                                       scalar=1.0 / (SL * SL), in1=x2[a3.j % 2][:, 2 * i:2 * i + 2, :],
                                                       op0=ALU.mult, op1=ALU.add).then_inc(result_ready, 1)
                    if c == 7 and a2.ends() and not now.there():
                        g = a2.group()
                        dve.wait_ge(r_hi_ready, g + 1)
                        dve.wait_ge(r_turned, g * 2)
                        nc.vector.tensor_tensor(r_lo[:, :, :], last_n[:, :, :], r_hi[:, :, :], ALU.subtract).then_inc(r_lo_ready, 1)
                    coming = Unit(B, MEASURED_IN.get(j, -1), U) if c == 7 else e
                    entry_step = c == 7 and j in MEASURED_IN and coming.there() or j == -BEFORE and c == 0
                    if entry_step:
                        ln = LN_IN[coming.j % 2]
                        n = coming.group()
                        dve.wait_ge(x_loaded[coming.j % 2], coming.turns_of_two() * 16)
                        wait(dve, in_rstd, (n - 1) * 2)
                        statistics(ln, x_in[coming.j % 2], in_stats)
                    if tail_step:
                        dve.wait_ge(y_stats, v.done(R, R))
                    if mix_step:
                        dve.wait_ge(u_stats, w.done(R, R))
                    if last_step:
                        dve.wait_ge(last_stats, a2.group() * R + R)
                    if entry_step:
                        dve.wait_ge(in_stats, coming.group() * R + R)
                    of, chunk = (v, C - 1) if c == 0 else (now, c - 1)
                    if of.there():
                        dve.wait_ge(act_hi_ready, of.done(C, chunk + 1))
                        nc.vector.scalar_tensor_tensor(out=act_lo[:, chunk % RING, :], in0=act32[:, chunk % RING, :], scalar=SA,
                                                       in1=act_hi[:, chunk % RING, :], op0=ALU.mult,
                                                       op1=ALU.subtract).then_inc(act_lo_ready, 1)
                    if tail_step:
                        aggregate(LN_Y, y_mv, v.done(R, R), y_var)
                    if mix_step:
                        aggregate(LN_U, u_mv, w.done(R, R), u_var, eps=EPS * SA ** 2)
                    if last_step:
                        aggregate(LN_LAST, last_mv, a2.group() * R + R, last_var, scale=SL ** -2)
                    if entry_step:
                        aggregate(ln, in_mv, coming.group() * R + R, in_var, scale=SA ** -2)
                    if c == 3 and j == -BEFORE:
                        dve.wait_ge(columns_in, 16 * 3)
                        nc.vector.tensor_scalar(g1_s[:, :, :], g1_c[:, :, :], SW, None, ALU.mult).then_inc(g1s_ready, 1)
                        dve.wait_ge(g1s_ready, 1)
                        prepare_w1(0, range(K))
                    if c == 7 and j == -2:
                        prepare_w2(0, range(K))
                    if c == 4 and j == -1:
                        for l in range(L):
                            prepare_b1(l)
                    if c == 7 and j == -1:
                        dve.wait_ge(rows_in, 16 * 5)
                        for row in (g2_r, beta2_r):
                            nc.vector.tensor_scalar(row[:, 0:L - 1, :], row[:, 0:L - 1, :], SA, None, ALU.mult).then_inc(rows_scaled, 1)
                    if c == 7 and now.fixed and B == 0:
                        for k in range(K):
                            if j - k in W1_SLOTS:
                                prepare_w1(W1_SLOTS[j - k], (k,))
                            if j - k in W2_SLOTS:
                                prepare_w2(W2_SLOTS[j - k], (k,))
                        if j == LAST_MAP_SLOT:
                            prepare_last()

            program(dve, body)

        @block.tensor
        def _(pe):
            def prepare(l):
                pe.wait_ge(columns_in, 16 * 3)
                pe.wait_ge(stage1_in[l % 2], 16 * (l // 2 + 1))
                for c in range(C):
                    for k in range(K):
                        mm = nc.tensor.matmul(ps_b1[l][:, c:c + 1], stage1[l % 2][:, k, c * P:(c + 1) * P], beta1_c[:, l, k:k + 1],
                                              start=(k == 0), stop=(k == K - 1))
                mm.then_inc(b1_summed, 1)

            def first_product(v, c):
                for k in range(K):
                    for n, (a, b) in enumerate(((w1_hi, 0), (w1_hi, 1), (w1_lo, 0))):
                        mm = nc.tensor.matmul(ps_h[c % 2][:, :], a[:, v.p, k, c * P:(c + 1) * P], ht[v.j % 2][:, b, k, :],
                                              start=(k == 0 and n == 0), stop=(k == K - 1 and n == 2))
                mm.then_inc(hidden, 1)

            def second_product(v, c):
                pe.wait_ge(act_lo_ready, v.done(C, c + 1))
                for r in range(R):
                    if c == 0 and r % 2 == 0:
                        wait(pe, y_ready, v.done(2, r // 2 - 1))
                    for n, (a, b) in enumerate(((act_hi, w2_hi), (act_hi, w2_lo), (act_lo, w2_hi))):
                        mm = nc.tensor.matmul(ps_f[r // 2][:, r % 2, :], a[:, c % RING, r * P:(r + 1) * P], b[:, v.p, c, :],
                                              start=(c == 0 and r % 2 == 0 and n == 0), stop=(c == C - 1 and n == 2),
                                              skip_group_check=True)
                    if r % 2:
                        mm.then_inc(second, 1)

            def turn(to_hi, hi, to_lo, lo, done):
                for to, of in ((to_hi, hi), (to_lo, lo)):
                    for r in range(R):
                        for k in range(K):
                            mm = nc.tensor.transpose(to[:, k, r * P:(r + 1) * P], of[:, r, k * P:(k + 1) * P], ident[:, :])
                    mm.then_inc(done, 1)

            ps_t_k = ps_t[:, :].rearrange("p (k r) -> p k r", k=K)
            pe.wait_ge(masks, MASK_STEPS)
            pe.wait_ge(halves_set, 1)

            def body(B, j):
                a3, a2, v, now, w, s, e = (Unit(B, j + i, U) for i in (-3, -2, -1, 0, 1, 2, 3))
                for c in range(C):
                    if now.there():
                        if c == 0:
                            pe.wait_ge(ht_hi_ready, now.done(1, 1))
                            pe.wait_ge(ht_lo_ready, now.done(1, 1))
                            if now.fixed and B == 0:
                                pe.wait_ge(w1_lo_ready, K * (now.p + 1))
                                pe.wait_ge(b1_ready, L)
                        wait(pe, act_ready, now.done(C, c - 1))
                        first_product(now, c)
                    if c == 0 and w.there():
                        pe.wait_ge(p_lo_ready, w.done(2, 2))
                        wait(pe, ht_lo_ready, upto(now, 1))
                        for i, of in enumerate((p_hi, p_lo)):
                            for r in range(R):
                                mm = nc.tensor.transpose(ps_t[:, (i * R + r) * P:(i * R + r + 1) * P], of[:, r, :], ident[:, :])
                        mm.then_inc(p_turned, 1)
                    if c == 1 and a3.ends():
                        g = a3.group()
                        pe.wait_ge(r_lo_ready, g + 1)
                        wait(pe, ht_hi_ready, upto(now, 1))
                        wait(pe, ht_lo_ready, upto(now, 1))
                        wait(pe, pt_ready, upto(w, 1))
                        turn(ps_s, r_hi, ps_t_k, r_lo, r_turned)
                    if c == 1 and w.there():
                        pe.wait_ge(pt_ready, w.done(1, 1))
                        pe.wait_ge(x_lo_ready, w.done(1, 1))
                        wait(pe, u_ready, w.done(R))
                        a4 = Unit(B, j - 4, U)
                        if a4.ends():
                            pe.wait_ge(result_ready, a4.group() * 2 + 2)
                        if a3.ends():
                            pe.wait_ge(counts_ready, a3.group() + 1)
                        for r in range(R):
                            for n, (a, b) in enumerate(((0, x_hi), (0, x_lo), (1, x_hi))):
                                mm = nc.tensor.matmul(ps_a[r // 2][:, r % 2, :], pt[:, a, r, :], b[:, r, :],
                                                      start=(n == 0), stop=(n == 2))
                            if r % 2:
                                mm.then_inc(mixed, 1)
                    if c == 2 and s.there():
                        pe.wait_ge(diag_ready, s.done(1, 1))
                        wait(pe, ht_hi_ready, upto(now, 1))
                        if a3.ends():
                            pe.wait_ge(rt_ready, a3.group() * 2 + 2)
                        nc.tensor.matmul(ps_s32[:, 0:R * N], blocks[:, :], diag[:, :, :].rearrange("p r n -> p (r n)"),
                                         start=True, stop=True).then_inc(spread, 1)
                    if c in (3, 4) and a3.ends():
                        g = a3.group()
                        pe.wait_ge(rt_ready, g * 2 + 2)
                        pe.wait_ge(counts_ready, g + 1)
                        wait(pe, result_ready, g * 2)
                        pe.wait_ge(wl_ready, 2)
                        wait(pe, u_ready, upto(w, R))
                        for r in HALVES[c - 3]:
                            tile = slice(r * P, (r + 1) * P)
                            for n, (a, b) in enumerate(((0, wl_hi), (0, wl_lo), (1, wl_hi))):
                                for k in range(K):
                                    nc.tensor.matmul(ps_a[r // 2][:, r % 2, :], rt[:, a, k, tile], b[:, k, :],
                                                     start=(n == 0 and k == 0), stop=False)
                            mm = nc.tensor.matmul(ps_a[r // 2][:, r % 2, :], counts[:, tile], lab_halves[:, :], start=False, stop=True)
                            if r % 2:
                                mm.then_inc(mapped, 1)
                    if c == 6 and w.there():
                        pe.wait_ge(h_lo_ready, w.done(1, 1))
                        wait(pe, scored, upto(s, R))
                        wait(pe, pt_ready, upto(w, 1))
                        if a3.ends():
                            pe.wait_ge(rt_ready, a3.group() * 2 + 2)
                        turn(ps_s, h_hi, ps_t_k, h_lo, h_turned)
                    if (j, c) in ((-BEFORE, 3), (1 - BEFORE, 3), (2 - BEFORE, 3)):
                        prepare(j + BEFORE)
                    if c == 7 and a2.ends():
                        g = a2.group()
                        if a3.ends() and now.there():
                            pe.wait_ge(result_ready, g * 2 - 1)
                        pe.wait_ge(onehot_ready, g * 2 + 2)
                        wait(pe, u_ready, upto(w, R))
                        for l in range(LABELS // 2):
                            mm = nc.tensor.matmul(ps_counts[now.there()], pick[:, l, :], onehot[:, l, :],
                                                  start=(l == 0), stop=(l == LABELS // 2 - 1))
                        mm.then_inc(counted, 1)
                    if c < FFN_LAG and v.there():
                        second_product(v, c + C - FFN_LAG)
                    if c >= FFN_LAG and now.there():
                        if c == FFN_LAG and now.fixed and B == 0:
                            pe.wait_ge(w2_lo_ready, K * (now.p + 1))
                        second_product(now, c - FFN_LAG)

            program(pe, body)


def kernel(x, adj, L0_gnn_attn_w, L0_gnn_attn_b, L0_gnn_W1, L0_gnn_b1, L0_gnn_W2, L0_gnn_b2, L0_gnn_g1, L0_gnn_beta1,
           L0_gnn_g2, L0_gnn_beta2, L1_gnn_weights, L1_gnn_bias):
    import concourse.bacc as bacc
    import numpy as np
    from concourse.bass_utils import run_bass_kernel_spmd

    x, adj = np.asarray(x), np.asarray(adj)
    graphs = P // N * R

    def by_partition(a):
        a = np.asarray(a)
        return a.reshape(a.shape[0], -1, P).transpose(2, 0, 1)

    def row(a):
        return np.asarray(a).reshape(1, -1)

    arrays = {
        "x": x.reshape(-1, D),
        "adj": adj.reshape(-1, N),
        "adj_t": adj.reshape(-1, graphs, N, N).transpose(0, 3, 1, 2).reshape(-1, N, ROWS),
        "attn_w": row(L0_gnn_attn_w),
        "attn_b": row(L0_gnn_attn_b),
        "w1": L0_gnn_W1,
        "b1": by_partition(L0_gnn_b1),
        "w2": L0_gnn_W2,
        "b2": row(L0_gnn_b2),
        "g1": by_partition(L0_gnn_g1),
        "g1_row": row(L0_gnn_g1),
        "beta1": by_partition(L0_gnn_beta1),
        "beta1_row": row(L0_gnn_beta1),
        "g2": row(L0_gnn_g2),
        "beta2": row(L0_gnn_beta2),
        "wl": np.asarray(L1_gnn_weights).transpose(2, 0, 1).reshape(K, P, -1, D).transpose(1, 0, 2, 3).reshape(P, -1, D),
        "lab": L1_gnn_bias,
    }
    arrays = {f"in_{n}": np.ascontiguousarray(a) for n, a in arrays.items()}
    nc = bacc.Bacc("TRN2", target_bir_lowering=False, num_devices=1)
    args = [nc.dram_tensor(n, a.shape, mybir.dt.from_np(a.dtype), kind="ExternalInput").ap() for n, a in arrays.items()]
    out = nc.dram_tensor("out", arrays["in_x"].shape, F32, kind="ExternalOutput").ap()
    gnn_block(nc, *args, out)
    got = run_bass_kernel_spmd(nc, [arrays], core_ids=[0]).results[0]["out"]
    return got.reshape(x.shape)
```
